# Optimizing a Trainium2 kernel written in Bass

```python
import numpy as np
import jax
import jax.numpy as jnp

def _softmax(x, axis=-1):
    return jax.nn.softmax(x, axis=axis)

def _gelu(x):
    return jax.nn.gelu(x, approximate=True)

def _silu(x):
    return jax.nn.silu(x)

def _sigmoid(x):
    return jax.nn.sigmoid(x)

def _layernorm(x, axis=-1, eps=1e-05):
    m = jnp.mean(x, axis=axis, keepdims=True)
    v = jnp.var(x, axis=axis, keepdims=True)
    return (x - m) / jnp.sqrt(v + eps)

def _scatter_add(tgt, idx, src, axis=0):
    return tgt.at[idx].add(src)

def _segment_sum(src, seg, n):
    return jax.ops.segment_sum(src, seg, n)
kernel_name = 'mk_metaformer_d1_conv_nchw256_r2_0886f8'

def setup_inputs(seed: int=0):
    np.random.seed(seed)
    _w = jnp.asarray

    def _rec_inputs():
        import jax
        import jax.numpy as jnp
        _gk = jax.random.key(seed)
        x = -0.0003929 + 0.9999 * jax.random.normal(jax.random.fold_in(_gk, 1), (16, 128, 32, 32), jnp.float32)
        return x
    x = _rec_inputs()

    def _L0_conv_setup():
        import jax, jax.numpy as jnp
        import numpy as np
        NUM_HEADS = 8
        HEAD_DIM = 32
        LATENT = NUM_HEADS * HEAD_DIM
        IN_CH = 128
        key = jax.random.key(seed)
        k1, k2, k3, k4 = jax.random.split(key, 4)
        b, c, h, w = (16, IN_CH, 32, 32)
        net = jax.random.normal(k1, (b, c, h, w), dtype=jnp.float32)
        w_qkv = jax.random.normal(k2, (3 * LATENT, c), dtype=jnp.float32) / np.sqrt(c)
        w_out = jax.random.normal(k3, (c, LATENT), dtype=jnp.float32) / np.sqrt(LATENT)
        b_out = jax.random.normal(k4, (c,), dtype=jnp.float32) * 0.01
        return {'net': net, 'w_qkv': w_qkv, 'w_out': w_out, 'b_out': b_out}
    _L0_conv_all = _L0_conv_setup()
    _L0_conv_in = {k: v for k, v in _L0_conv_all.items() if k in ('w_qkv', 'w_out', 'b_out')}
    del _L0_conv_all

    def _L0_ffn_setup():
        import jax, jax.numpy as jnp
        import numpy as np
        BN_EPS = 0.001

        def _bn(h, g, b, m, v):
            return g * (h - m) * jax.lax.rsqrt(v + BN_EPS) + b
        key = jax.random.key(seed)
        ks = jax.random.split(key, 8)
        B, F, Df = (128, 32, 128)
        E, H, D = (8, 128, 128)
        s1 = 1.0 / np.sqrt(Df)
        s2 = 1.0 / np.sqrt(H)
        return {'x': jax.random.normal(ks[0], (B, F, Df), jnp.float32), 'Wr': jax.random.normal(ks[1], (Df, E), jnp.float32) * s1, 'br': jnp.zeros((E,), jnp.float32), 'W1': jax.random.normal(ks[2], (E, Df, H), jnp.float32) * s1, 'b1': jnp.zeros((E, H), jnp.float32), 'g1': jnp.ones((E, H), jnp.float32), 'be1': jnp.zeros((E, H), jnp.float32), 'm1': jnp.zeros((E, H), jnp.float32), 'v1': jnp.ones((E, H), jnp.float32), 'W2': jax.random.normal(ks[3], (E, H, H), jnp.float32) * s2, 'b2': jnp.zeros((E, H), jnp.float32), 'g2': jnp.ones((E, H), jnp.float32), 'be2': jnp.zeros((E, H), jnp.float32), 'm2': jnp.zeros((E, H), jnp.float32), 'v2': jnp.ones((E, H), jnp.float32), 'Wo': jax.random.normal(ks[4], (E, H, D), jnp.float32) * s2, 'bo': jnp.zeros((E, D), jnp.float32)}
    _L0_ffn_all = _L0_ffn_setup()
    _L0_ffn_in = {k: v for k, v in _L0_ffn_all.items() if k in ('Wr', 'br', 'W1', 'b1', 'g1', 'be1', 'm1', 'v1', 'W2', 'b2', 'g2', 'be2', 'm2', 'v2', 'Wo', 'bo')}
    del _L0_ffn_all
    return {'x': x, 'L0_conv_w_qkv': _L0_conv_in['w_qkv'], 'L0_conv_w_out': _L0_conv_in['w_out'], 'L0_conv_b_out': _L0_conv_in['b_out'], 'L0_ffn_Wr': _L0_ffn_in['Wr'], 'L0_ffn_br': _L0_ffn_in['br'], 'L0_ffn_W1': _L0_ffn_in['W1'], 'L0_ffn_b1': _L0_ffn_in['b1'], 'L0_ffn_g1': _L0_ffn_in['g1'], 'L0_ffn_be1': _L0_ffn_in['be1'], 'L0_ffn_m1': _L0_ffn_in['m1'], 'L0_ffn_v1': _L0_ffn_in['v1'], 'L0_ffn_W2': _L0_ffn_in['W2'], 'L0_ffn_b2': _L0_ffn_in['b2'], 'L0_ffn_g2': _L0_ffn_in['g2'], 'L0_ffn_be2': _L0_ffn_in['be2'], 'L0_ffn_m2': _L0_ffn_in['m2'], 'L0_ffn_v2': _L0_ffn_in['v2'], 'L0_ffn_Wo': _L0_ffn_in['Wo'], 'L0_ffn_bo': _L0_ffn_in['bo']}

def reference(x, L0_conv_w_qkv, L0_conv_w_out, L0_conv_b_out, L0_ffn_Wr, L0_ffn_br, L0_ffn_W1, L0_ffn_b1, L0_ffn_g1, L0_ffn_be1, L0_ffn_m1, L0_ffn_v1, L0_ffn_W2, L0_ffn_b2, L0_ffn_g2, L0_ffn_be2, L0_ffn_m2, L0_ffn_v2, L0_ffn_Wo, L0_ffn_bo):
    import jax
    import jax.numpy as jnp

    def _L0_conv_ref(net, w_qkv, w_out, b_out):
        import jax, jax.numpy as jnp
        import numpy as np
        NUM_HEADS = 8
        HEAD_DIM = 32
        LATENT = NUM_HEADS * HEAD_DIM
        IN_CH = 128
        b, c, h, w = net.shape
        n = h * w
        qkv = jnp.einsum('bchw,oc->bohw', net, w_qkv).reshape(b, 3, NUM_HEADS, HEAD_DIM, n)
        q, k, v = (qkv[:, 0], qkv[:, 1], qkv[:, 2])
        k = jax.nn.softmax(k, axis=-1)
        context = jnp.einsum('bhdn,bhen->bhde', k, v)
        out = jnp.einsum('bhde,bhdn->bhen', context, q)
        out = out.reshape(b, LATENT, h, w)
        out = jnp.einsum('blhw,cl->bchw', out, w_out) + b_out[None, :, None, None]
        return out

    def _L0_ffn_ref(x, Wr, br, W1, b1, g1, be1, m1, v1, W2, b2, g2, be2, m2, v2, Wo, bo):
        import jax, jax.numpy as jnp
        import numpy as np
        BN_EPS = 0.001

        def _bn(h, g, b, m, v):
            return g * (h - m) * jax.lax.rsqrt(v + BN_EPS) + b
        feat = jnp.mean(x, axis=0)
        w = jax.nn.softmax(feat @ Wr + br, axis=-1)
        h = jnp.einsum('bfd,edh->bfeh', x, W1) + b1
        h = jax.nn.relu(_bn(h, g1, be1, m1, v1))
        h = jnp.einsum('bfeh,ehk->bfek', h, W2) + b2
        h = jax.nn.relu(_bn(h, g2, be2, m2, v2))
        y = jnp.einsum('bfeh,ehd->bfed', h, Wo) + bo
        return jnp.einsum('bfed,fe->bfd', y, w)

    def _gn(v, G=32, eps=1e-05):
        B_, C_, H_, W_ = v.shape
        g = v.reshape(B_, G, C_ // G, H_, W_)
        m = jnp.mean(g, axis=(2, 3, 4), keepdims=True)
        s = jnp.var(g, axis=(2, 3, 4), keepdims=True)
        return ((g - m) / jnp.sqrt(s + eps)).reshape(v.shape)

    def _ln_c(v, eps=1e-06):
        m = jnp.mean(v, axis=1, keepdims=True)
        s = jnp.var(v, axis=1, keepdims=True)
        return (v - m) / jnp.sqrt(s + eps)

    def _ln_t(v, eps=1e-05):
        m = jnp.mean(v, axis=-1, keepdims=True)
        s = jnp.var(v, axis=-1, keepdims=True)
        return (v - m) / jnp.sqrt(s + eps)

    def _to_tokens(v):
        B_, C_, H_, W_ = v.shape
        return v.reshape(B_, C_, H_ * W_).transpose(0, 2, 1)

    def _from_tokens(t, like):
        B_, C_, H_, W_ = like.shape
        return t.transpose(0, 2, 1).reshape(B_, C_, H_, W_)
    x = x + _L0_conv_ref(_ln_c(x), L0_conv_w_qkv, L0_conv_w_out, L0_conv_b_out)
    t = _to_tokens(x)
    t = t + _L0_ffn_ref(_ln_t(t), L0_ffn_Wr, L0_ffn_br, L0_ffn_W1, L0_ffn_b1, L0_ffn_g1, L0_ffn_be1, L0_ffn_m1, L0_ffn_v1, L0_ffn_W2, L0_ffn_b2, L0_ffn_g2, L0_ffn_be2, L0_ffn_m2, L0_ffn_v2, L0_ffn_Wo, L0_ffn_bo)
    x = _from_tokens(t, x)
    return x

_drawn_inputs = setup_inputs


def setup_inputs(seed=0):
    import zlib

    import numpy as np

    out = dict(_drawn_inputs(seed))
    spreads = {'L0_ffn_br': (0.0, 0.305),
     'L0_ffn_b1': (0.0, 0.482),
     'L0_ffn_g1': (1.0, 0.2),
     'L0_ffn_be1': (0.0, 0.5),
     'L0_ffn_m1': (0.0, 0.474),
     'L0_ffn_v1': (1.0, 0.6),
     'L0_ffn_b2': (0.0, 0.349),
     'L0_ffn_g2': (1.0, 0.2),
     'L0_ffn_be2': (0.0, 0.369),
     'L0_ffn_m2': (0.0, 0.357),
     'L0_ffn_v2': (1.0, 0.6),
     'L0_ffn_bo': (0.0, 0.1)}
    factors = {'L0_conv_b_out': 6.122}
    for name, (base, spread) in spreads.items():
        noise = np.random.default_rng([zlib.crc32(name.encode()), seed]).standard_normal(out[name].shape)
        drawn = base * np.exp(spread * noise) if base else spread * noise
        out[name] = jnp.asarray(drawn.astype(out[name].dtype))
    for name, factor in factors.items():
        out[name] = (out[name] * factor).astype(out[name].dtype)
    return out
```

```python
from contextlib import ExitStack

import numpy as np

import concourse.bass as bass
from concourse import mybir

F32 = mybir.dt.float32
F32R = mybir.dt.float32r
ALU = mybir.AluOpType
ACT = mybir.ActivationFunctionType
AX = mybir.AxisListType

IMAGES, C, SIDE = 16, 128, 32
PIXELS = SIDE * SIDE
CHUNKS = PIXELS // 128
HEADS, HEAD_DIM = 8, 32
LATENT = HEADS * HEAD_DIM
EXPERTS, HIDDEN = 8, 128
BANK = 512
LN_C_EPS, LN_T_EPS, BN_EPS = 1e-6, 1e-5, 1e-3
G1, V1, B1, M1, BE1, G2, V2, B2, M2, BE2 = range(10)
S1, T1, S2, T2 = range(4)
QUARTER_C, ROOT_C, MINUS_HALF, LN_C_EPS_C, LN_T_EPS_C = range(5)
CONSTANTS = {QUARTER_C: C / 4, ROOT_C: C ** 0.5, MINUS_HALF: -0.5, LN_C_EPS_C: C * LN_C_EPS, LN_T_EPS_C: C * LN_T_EPS}


def wait(engine, semaphore, count):
    if not isinstance(count, int) or count > 0:
        engine.wait_ge(semaphore, count)


def metaformer_kernel(nc, x, w_qkv, w_out, b_out, Wr, br, W1, W2, Wo, small, bo, ident_in, heads_in, sel_in, out):
    x1_dram = nc.dram_tensor("x1_scratch", [IMAGES, C, PIXELS], F32, kind="Internal").ap()
    xn2_dram = nc.dram_tensor("xn2_scratch", [IMAGES, C, PIXELS], F32, kind="Internal").ap()

    with ExitStack() as whole:
        def keep(name, shape, dt=F32):
            return whole.enter_context(nc.sbuf_tensor(name, shape, dt))

        psum = whole.enter_context(nc.psum_tensor("psum", [128, 8, BANK], F32))

        def banks(first, n):
            return psum[:, first:first + n, :].rearrange("p b n -> p (b n)")

        w_hi = keep("w_hi", [128, 3, EXPERTS, 128], F32R)
        w_lo = keep("w_lo", [128, 3, EXPERTS, 128], F32R)
        ident = keep("ident", [128, 128])
        t2 = keep("t2", [HIDDEN, EXPERTS])
        bo_sb = keep("bo_sb", [EXPERTS, C])
        wr_sb = keep("wr_sb", [C, EXPERTS])
        br_sb = keep("br_sb", [128, EXPERTS])
        feat = keep("feat", [128, CHUNKS, C])

        attention_block(nc, psum, banks, x, w_qkv, w_out, b_out, Wr, br, W1, W2, Wo, small, bo,
                        ident_in, heads_in, sel_in, x1_dram, xn2_dram,
                        w_hi, w_lo, ident, t2, bo_sb, wr_sb, br_sb, feat)
        expert_block(nc, banks, x1_dram, xn2_dram, w_hi, w_lo, ident, t2, bo_sb, wr_sb, br_sb, feat, out)


def attention_block(nc, psum, banks, x, w_qkv, w_out, b_out, Wr, br, W1, W2, Wo, small, bo,
                    ident_in, heads_in, sel_in, x1_dram, xn2_dram,
                    w_hi, w_lo, ident, t2, bo_sb, wr_sb, br_sb, feat):
    with ExitStack() as ctx:
        def sb(name, shape, dt=F32):
            return ctx.enter_context(nc.sbuf_tensor(name, shape, dt))

        def sem(name):
            return ctx.enter_context(nc.semaphore(name))

        heads = sb("heads", [128, 128])
        sel = sb("sel", [EXPERTS, EXPERTS, 128])
        wqkv_sb = sb("wqkv_sb", [128, 6, C])
        wout_sb = sb("wout_sb", [C, LATENT])
        bout_sb = sb("bout_sb", [C, 1])
        wkT_hi = sb("wkT_hi", [C, LATENT], F32R)
        wkT_lo = sb("wkT_lo", [C, LATENT], F32R)
        wvT = sb("wvT", [C, LATENT])
        woutT = sb("woutT", [128, 2, C])
        w_raw = sb("w_raw", [128, 3, EXPERTS, 128])
        small_sb = sb("small_sb", [EXPERTS, 10, HIDDEN])
        bn_std = sb("bn_std", [EXPERTS, 2, HIDDEN])
        bn_tmp = sb("bn_tmp", [EXPERTS, 2, HIDDEN])
        rows = sb("rows", [EXPERTS, 4, HIDDEN])
        minus_mean = sb("minus_mean", [128, 128])
        const = sb("const", [128, len(CONSTANTS), CHUNKS])
        half_neg = sb("half_neg", [128, HIDDEN])
        x_in = [sb(f"x_in{p}", [C, PIXELS]) for p in range(2)]
        x_res = [sb(f"x_res{p}", [C, PIXELS]) for p in range(2)]
        xnT = [sb(f"xnT{p}", [128, CHUNKS, C]) for p in range(2)]
        xn_hi = [sb(f"xn_hi{p}", [C, PIXELS], F32R) for p in range(2)]
        xn_lo = [sb(f"xn_lo{p}", [C, PIXELS], F32R) for p in range(2)]
        ek = [sb(f"ek{j}", [128, PIXELS]) for j in range(2)]
        ekT = [sb(f"ekT{j}", [128, CHUNKS, 128]) for j in range(2)]
        negmax = sb("negmax", [128, 2])
        rawmax = sb("rawmax", [128, 2])
        sums = [sb(f"sums{p}", [128, 2]) for p in range(2)]
        rsum = sb("rsum", [128, 2])
        gT = sb("gT", [C, LATENT])
        ctxT = sb("ctxT", [128, 2, 128])
        y_sb = sb("y_sb", [128, 2, C])
        mT_hi = sb("mT_hi", [C, C], F32R)
        mT_lo = sb("mT_lo", [C, C], F32R)
        xn2T = sb("xn2T", [128, CHUNKS, C])
        xn2 = [sb(f"xn2_{p}", [C, PIXELS]) for p in range(2)]
        st = [sb(f"st{k}", [128, CHUNKS, 6]) for k in range(2)]
        ln = [sb(f"ln{k}", [128, 8, CHUNKS]) for k in range(2)]

        p_tok, p_chan, p_k, p_e, p_g = banks(0, 2), banks(2, 2), banks(4, 2), banks(6, 1), banks(7, 1)

        attn_w = sem("attn_w")
        expert_w = sem("expert_w")
        in_loaded = [sem(f"in_loaded{p}") for p in range(2)]
        res_loaded = [sem(f"res_loaded{p}") for p in range(2)]
        x1_stored = [sem(f"x1_stored{p}") for p in range(2)]
        xn2_stored = [sem(f"xn2_stored{p}") for p in range(2)]
        const_set = sem("const_set")
        wT_done, wk_hi_done, wT_moved = sem("wT_done"), sem("wk_hi_done"), sem("wT_moved")
        bn_step, rows_done, bcast_done, scaled = sem("bn_step"), sem("rows_done"), sem("bcast_done"), sem("scaled")
        shift_done, w1_shifted, w_hi_done, w_split = sem("shift_done"), sem("w1_shifted"), sem("w_hi_done"), sem("w_split")
        k_done, ctx_done, tx_done, y_done = sem("k_done"), sem("ctx_done"), sem("tx_done"), sem("y_done")
        m_done, mx_done, e_done, g_done = sem("m_done"), sem("mx_done"), sem("e_done"), sem("g_done")
        xnt_done, x1t_done, xn2t_done = sem("xnt_done"), sem("x1t_done"), sem("xn2t_done")
        xn2_moved, exp_done, m_hi_done, norm1_done = sem("xn2_moved"), sem("exp_done"), sem("m_hi_done"), sem("norm1_done")
        e0_moved, xn_hi_done, norm2_done = sem("e0_moved"), sem("xn_hi_done"), sem("norm2_done")
        g_moved, max_done, negmax_done, ctx_moved = sem("g_moved"), sem("max_done"), sem("negmax_done"), sem("ctx_moved")
        rsum_done, y_moved, stats1_done, m_lo_done = sem("rsum_done"), sem("y_moved"), sem("stats1_done"), sem("m_lo_done")
        x1_done, e1_moved, xn_lo_done, stats2_done = sem("x1_done"), sem("e1_moved"), sem("xn_lo_done"), sem("stats2_done")
        ln_step, ln1_done, ln2_done, feat_done = sem("ln_step"), sem("ln1_done"), sem("ln2_done"), sem("feat_done")

        LN_STEPS = 10

        def rounds(engine, step):
            def valid(t):
                return dict(a=t + 1 < IMAGES, b=0 <= t < IMAGES, c=0 <= t - 1 < IMAGES, d=0 <= t - 2 < IMAGES)
            for t in range(-1, 4):
                step(t, t % 2, **valid(t))
            with engine.Fori(0, (IMAGES - 6) // 2) as i:
                for p in range(2):
                    step(2 * i + (4 + p), p, a=True, b=True, c=True, d=True)
            for t in range(IMAGES - 2, IMAGES + 2):
                step(t, t % 2, **valid(t))

        block = ctx.enter_context(nc.Block())

        @block.sync
        def _(sp):
            sp.dma_start(ident[:], ident_in).then_inc(attn_w, 16)
            sp.dma_start(x_in[0][:], x[0]).then_inc(in_loaded[0], 16)
            sp.dma_start(wqkv_sb[:], w_qkv.rearrange("(t p) c -> p t c", p=128)).then_inc(attn_w, 16)
            sp.dma_start(wout_sb[:], w_out).then_inc(attn_w, 16)
            sp.dma_start(heads[:], heads_in).then_inc(attn_w, 16)
            sp.dma_start(bout_sb[:], b_out).then_inc(attn_w, 16)
            sp.dma_start(x_in[1][:], x[1]).then_inc(in_loaded[1], 16)
            sp.dma_start(small_sb[:], small).then_inc(expert_w, 16)
            sp.dma_start(sel[:], sel_in).then_inc(expert_w, 16)
            sp.dma_start(bo_sb[:], bo).then_inc(expert_w, 16)
            sp.dma_start(wr_sb[:], Wr).then_inc(expert_w, 16)
            sp.dma_start(br_sb[:], br).then_inc(expert_w, 16)
            for k, w in enumerate((W1, W2, Wo)):
                sp.dma_start(w_raw[:, k], w.rearrange("e c h -> c e h")).then_inc(expert_w, 16)

            def step(t, p, a, b, c, d):
                q = 1 - p
                if isinstance(t, int) and not 0 <= t < IMAGES - 2:
                    pass
                else:
                    sp.wait_ge(tx_done, t + 1)
                    sp.dma_start(x_in[p][:], x[t + 2]).then_inc(in_loaded[p], 16)
                if b:
                    if not isinstance(t, int) or t >= 2:
                        sp.wait_ge(x1t_done, t - 1)
                        sp.wait_ge(x1_stored[p], 8 * t - 8 * p)
                    sp.dma_start(x_res[p][:], x[t]).then_inc(res_loaded[p], 16)
                if d:
                    sp.wait_ge(xn2_moved, t - 1)
                    sp.dma_start(xn2_dram[t - 2], xn2[p][:]).then_inc(xn2_stored[p], 16)
                if c:
                    sp.wait_ge(x1_done, t)
                    sp.dma_start(x1_dram[t - 1], x_res[q][:]).then_inc(x1_stored[q], 16)

            rounds(sp, step)
            for p in range(2):
                sp.wait_ge(x1_stored[p], 16 * (IMAGES // 2))
                sp.wait_ge(xn2_stored[p], 16 * (IMAGES // 2))

        @block.tensor
        def _(pe):
            pe.wait_ge(attn_w, 5 * 16)
            for k in range(4):
                pe.transpose(p_tok[:, 128 * k:128 * (k + 1)], wqkv_sb[:, 2 + k, :], ident[:])
            for j in range(2):
                mm = pe.transpose(p_tok[:, BANK + 128 * j:BANK + 128 * (j + 1)], wout_sb[:, 128 * j:128 * (j + 1)], ident[:])
            mm.then_inc(wT_done, 1)

            def step(t, p, a, b, c, d):
                q = 1 - p
                if b:
                    k_half(t, p, 0)
                if c:
                    pe.wait_ge(g_moved, t)
                    for j in range(2):
                        half = slice(128 * j, 128 * (j + 1))
                        mm = pe.matmul(p_g[:, 256 + 128 * j:256 + 128 * (j + 1)], wvT[:, half], gT[:, half], start=True, stop=True)
                    mm.then_inc(ctx_done, 1)
                if d:
                    pe.wait_ge(norm2_done, t - 1)
                    if b:
                        pe.wait_ge(xn_lo_done, t + 1)
                    for n in range(CHUNKS):
                        mm = pe.transpose(p_chan[:, 128 * n:128 * (n + 1)], xn2T[:, n, :], ident[:])
                    mm.then_inc(xn2t_done, 1)
                if c:
                    pe.wait_ge(ctx_moved, t)
                    for j in range(2):
                        mm = pe.matmul(p_g[:, 128 * j:128 * (j + 1)], ctxT[:, j, :], woutT[:, j, :], start=True, stop=True)
                    mm.then_inc(y_done, 1)
                if a:
                    pe.wait_ge(in_loaded[q], 8 * t + (24 if p else 16))
                    if isinstance(t, int) and t == -1:
                        pe.wait_ge(wT_moved, 1)
                    wait(pe, norm2_done, t - 1)
                    for n in range(CHUNKS):
                        mm = pe.transpose(p_tok[:, 128 * n:128 * (n + 1)], x_in[q][:, 128 * n:128 * (n + 1)], ident[:])
                    mm.then_inc(tx_done, 1)
                if c:
                    pe.wait_ge(y_moved, t)
                    for j in range(2):
                        mm = pe.matmul(p_g[:, 256:384], wqkv_sb[:, j, :], y_sb[:, j, :], start=j == 0, stop=j == 1)
                    mm.then_inc(m_done, 1)
                    pe.wait_ge(m_lo_done, t)
                    wait(pe, xn2_moved, t - 1)
                    for n in range(2):
                        cols = slice(BANK * n, BANK * (n + 1))
                        pe.matmul(p_chan[:, cols], mT_hi[:], xn_hi[q][:, cols], start=True, stop=False)
                        pe.matmul(p_chan[:, cols], mT_hi[:], xn_lo[q][:, cols], start=False, stop=False)
                        mm = pe.matmul(p_chan[:, cols], mT_lo[:], xn_hi[q][:, cols], start=False, stop=True)
                    mm.then_inc(mx_done, 1)
                if b:
                    k_half(t, p, 1)
                    turn_e(t, 0, 0)
                    turn_e(t, 0, 1)
                    add_g(t, p, 0, 0)
                    add_g(t, p, 0, 1)
                if a:
                    pe.wait_ge(norm1_done, t + 2)
                    wait(pe, x1_done, t)
                    for n in range(CHUNKS):
                        mm = pe.transpose(p_chan[:, 128 * n:128 * (n + 1)], xnT[q][:, n, :], ident[:])
                    mm.then_inc(xnt_done, 1)
                if c:
                    pe.wait_ge(x1_done, t)
                    if not isinstance(t, int) or t < IMAGES:
                        pe.wait_ge(norm1_done, min(t + 2, IMAGES) if isinstance(t, int) else t + 2)
                    for n in range(CHUNKS):
                        mm = pe.transpose(p_tok[:, 128 * n:128 * (n + 1)], x_res[q][:, 128 * n:128 * (n + 1)], ident[:])
                    mm.then_inc(x1t_done, 1)
                if b:
                    turn_e(t, 1, 0)
                    turn_e(t, 1, 1)
                    add_g(t, p, 1, 0)
                    add_g(t, p, 1, 1)

            def k_half(t, p, j):
                half = slice(128 * j, 128 * (j + 1))
                if j == 0:
                    pe.wait_ge(xn_lo_done, t + 1)
                wait(pe, exp_done, 2 * t + j)
                for w, xs in ((wkT_hi, xn_hi), (wkT_lo, xn_hi), (wkT_hi, xn_lo)):
                    for n in range(2):
                        cols = slice(BANK * n, BANK * (n + 1))
                        mm = pe.matmul(p_k[:, cols], w[:, half], xs[p][:, cols],
                                       start=w is wkT_hi and xs is xn_hi, stop=xs is xn_lo, skip_group_check=True)
                mm.then_inc(k_done, 1)

            def turn_e(t, j, h):
                if h == 0:
                    pe.wait_ge(exp_done, 2 * t + j + 1)
                if (j, h) == (0, 0):
                    wait(pe, e1_moved, 2 * t)
                elif j == 0 or h == 0:
                    pe.wait_ge(e0_moved, 2 * t + (1 if j == 0 else 2))
                else:
                    pe.wait_ge(e1_moved, 2 * t + 1)
                for n in range(4):
                    chunk = 4 * h + n
                    mm = pe.transpose(p_e[:, 128 * n:128 * (n + 1)], ek[j][:, 128 * chunk:128 * (chunk + 1)], ident[:])
                mm.then_inc(e_done, 1)

            def add_g(t, p, j, h):
                pe.wait_ge((e0_moved, e1_moved)[j], 2 * t + h + 1)
                for n in range(4):
                    chunk = 4 * h + n
                    mm = pe.matmul(p_g[:, 128 * j:128 * (j + 1)], xnT[p][:, chunk, :], ekT[j][:, chunk, :],
                                   start=chunk == 0, stop=chunk == CHUNKS - 1)
                if (j, h) == (1, 1):
                    mm.then_inc(g_done, 1)

            rounds(pe, step)

            pe.wait_ge(rows_done, 1)
            pe.wait_ge(expert_w, 8 * 16)
            pe.wait_ge(norm2_done, IMAGES)
            for dst, row in ((p_tok, S1), (p_k, S2)):
                for e in range(EXPERTS):
                    pe.matmul(dst[:, 128 * e:128 * (e + 1)], sel[:, e, :], rows[:, row, :], start=True, stop=True)
            pe.transpose(p_g[:, 0:EXPERTS], rows[:, T2, :], ident[0:EXPERTS, 0:EXPERTS]).then_inc(bcast_done, 1)
            pe.wait_ge(scaled, 1)
            pe.wait_ge(xn2_moved, IMAGES)
            for e in range(EXPERTS):
                pe.matmul(p_chan[:, 128 * e:128 * (e + 1)], minus_mean[:], w_raw[:, 0, e, :], start=True, stop=False)
                mm = pe.matmul(p_chan[:, 128 * e:128 * (e + 1)], sel[:, e, :], rows[:, T1, :], start=False, stop=True)
            mm.then_inc(shift_done, 1)

        @block.scalar
        def _(act):
            act.wait_ge(wT_done, 1)
            nc.scalar.copy(wkT_hi[:], p_tok[:, 0:LATENT]).then_inc(wk_hi_done, 1)

            def step(t, p, a, b, c, d):
                q = 1 - p
                if d:
                    act.wait_ge(xn2t_done, t - 1)
                    if not isinstance(t, int) or t >= 4:
                        act.wait_ge(xn2_stored[p], 8 * t - 16 - 8 * p)
                    nc.scalar.activation(xn2[p][:], p_chan, ACT.Copy, bias=1.0).then_inc(xn2_moved, 1)
                if b:
                    exp_half(t, p, 0)
                if c:
                    act.wait_ge(m_done, t)
                    wait(act, mx_done, t - 1)
                    nc.scalar.copy(mT_hi[:], p_g[:, 256:384]).then_inc(m_hi_done, 1)
                if a:
                    act.wait_ge(ln1_done, t + 2)
                    wait(act, g_done, t)
                    for n in range(CHUNKS):
                        ins = nc.scalar.activation(xnT[q][:, n, :], p_tok[:, 128 * n:128 * (n + 1)], ACT.Identity,
                                                   scale=ln[0][:, 6, n:n + 1], bias=ln[0][:, 7, n:n + 1])
                    ins.then_inc(norm1_done, 1)
                if b:
                    for h in range(2):
                        act.wait_ge(e_done, 4 * t + h + 1)
                        wait(act, g_done, t)
                        nc.scalar.copy(ekT[0][:, 4 * h:4 * h + 4, :].rearrange("p n d -> p (n d)"), p_e).then_inc(e0_moved, 1)
                    exp_half(t, p, 1)
                if a:
                    act.wait_ge(xnt_done, t + 2)
                    wait(act, mx_done, t)
                    nc.scalar.copy(xn_hi[q][:], p_chan).then_inc(xn_hi_done, 1)
                if c:
                    act.wait_ge(ln2_done, t)
                    wait(act, xn2t_done, t - 1)
                    wait(act, feat_done, t - 1)
                    for n in range(CHUNKS):
                        ins = nc.scalar.activation(xn2T[:, n, :], p_tok[:, 128 * n:128 * (n + 1)], ACT.Identity,
                                                   scale=ln[1][:, 6, n:n + 1], bias=ln[1][:, 7, n:n + 1])
                    ins.then_inc(norm2_done, 1)

            def exp_half(t, p, j):
                act.wait_ge(negmax_done, 2 * t + j + 1)
                wait(act, e_done, 4 * t + 2 * j - 2)
                if j == 0:
                    wait(act, rsum_done, t - 1)
                nc.scalar.activation(ek[j][:], p_k, ACT.Exp, bias=negmax[:, j:j + 1],
                                     accum_out=sums[p][:, j:j + 1]).then_inc(exp_done, 1)

            rounds(act, step)

            act.wait_ge(scaled, 2)
            for k in (2, 1, 0):
                if k == 0:
                    act.wait_ge(w1_shifted, 1)
                nc.scalar.copy(w_hi[:, k].rearrange("p e h -> p (e h)"),
                               w_raw[:, k].rearrange("p e h -> p (e h)")).then_inc(w_hi_done, 1)

        @block.vector
        def _(dve):
            dve.wait_ge(wk_hi_done, 1)
            nc.vector.tensor_tensor(wkT_lo[:], p_tok[:, 0:LATENT], wkT_hi[:].bitcast(F32), ALU.subtract)
            nc.vector.tensor_copy(wvT[:], p_tok[:, LATENT:2 * LATENT])
            nc.vector.tensor_copy(woutT[:].rearrange("p j c -> p (j c)"), p_tok[:, BANK:BANK + LATENT]).then_inc(wT_moved, 1)

            def step(t, p, a, b, c, d):
                q = 1 - p
                if c:
                    dve.wait_ge(g_done, t)
                    wait(dve, ctx_done, t - 1)
                    nc.vector.tensor_copy(gT[:], p_g[:, 0:LATENT]).then_inc(g_moved, 1)
                if b:
                    head_max(t, 0)
                if c:
                    dve.wait_ge(ctx_done, t)
                    wait(dve, y_done, t - 1)
                    for j in range(2):
                        ins = nc.vector.tensor_tensor(ctxT[:, j, :], p_g[:, 256 + 128 * j:256 + 128 * (j + 1)], heads[:], ALU.mult)
                    ins.then_inc(ctx_moved, 1)
                    dve.wait_ge(exp_done, 2 * t)
                    nc.vector.reciprocal(rsum[:], sums[q][:]).then_inc(rsum_done, 1)
                    dve.wait_ge(rsum_done, t)
                    dve.wait_ge(y_done, t)
                    wait(dve, m_done, t - 1)
                    for j in range(2):
                        ins = nc.vector.tensor_scalar(y_sb[:, j, :], p_g[:, 128 * j:128 * (j + 1)], rsum[:, j:j + 1], None, ALU.mult)
                    ins.then_inc(y_moved, 1)
                if a:
                    dve.wait_ge(tx_done, t + 2)
                    wait(dve, ln1_done, t + 1)
                    for n in range(CHUNKS):
                        ins = nc.vector.bn_stats(st[0][:, n, :], p_tok[:, 128 * n:128 * (n + 1)])
                    ins.then_inc(stats1_done, 1)
                if c:
                    dve.wait_ge(m_hi_done, t)
                    nc.vector.tensor_tensor(mT_lo[:], p_g[:, 256:384], mT_hi[:].bitcast(F32), ALU.subtract).then_inc(m_lo_done, 1)
                    dve.wait_ge(mx_done, t)
                    dve.wait_ge(res_loaded[q], 8 * t + (0 if q else 8))
                    nc.vector.scalar_tensor_tensor(out=x_res[q][:], in0=p_chan, scalar=bout_sb[:, 0:1], in1=x_res[q][:],
                                                   op0=ALU.add, op1=ALU.add).then_inc(x1_done, 1)
                if b:
                    head_max(t, 1)
                    for h in range(2):
                        dve.wait_ge(e_done, 4 * t + h + 3)
                        nc.vector.tensor_copy(ekT[1][:, 4 * h:4 * h + 4, :].rearrange("p n d -> p (n d)"), p_e).then_inc(e1_moved, 1)
                if a:
                    dve.wait_ge(xn_hi_done, t + 2)
                    nc.vector.tensor_tensor(xn_lo[q][:], p_chan, xn_hi[q][:].bitcast(F32), ALU.subtract).then_inc(xn_lo_done, 1)
                if c:
                    dve.wait_ge(x1t_done, t)
                    wait(dve, ln2_done, t - 1)
                    for n in range(CHUNKS):
                        ins = nc.vector.bn_stats(st[1][:, n, :], p_tok[:, 128 * n:128 * (n + 1)])
                    ins.then_inc(stats2_done, 1)

            def head_max(t, j):
                dve.wait_ge(k_done, 2 * t + j + 1)
                wait(dve, exp_done, 2 * t + j - 1)
                nc.vector.tensor_reduce(rawmax[:, j:j + 1], p_k, AX.X, ALU.max).then_inc(max_done, 1)
                dve.wait_ge(max_done, 2 * t + j + 1)
                nc.vector.tensor_scalar(negmax[:, j:j + 1], rawmax[:, j:j + 1], -1.0, None, ALU.mult).then_inc(negmax_done, 1)

            rounds(dve, step)

            dve.wait_ge(bcast_done, 1)
            flat = [w_raw[:, k].rearrange("p e h -> p (e h)") for k in range(3)]
            nc.vector.tensor_tensor(flat[0], flat[0], p_tok, ALU.mult).then_inc(scaled, 1)
            nc.vector.tensor_tensor(flat[1], flat[1], p_k, ALU.mult)
            nc.vector.tensor_copy(t2[:], p_g[:, 0:EXPERTS]).then_inc(scaled, 1)
            dve.wait_ge(shift_done, 1)
            dve.wait_ge(scaled, 2)
            nc.vector.tensor_tensor(flat[0], flat[0], p_chan, ALU.add).then_inc(w1_shifted, 1)
            for n, k in enumerate((2, 1, 0)):
                dve.wait_ge(w_hi_done, n + 1)
                if k == 0:
                    dve.wait_ge(w1_shifted, 1)
                nc.vector.tensor_tensor(w_lo[:, k].rearrange("p e h -> p (e h)"), flat[k],
                                        w_hi[:, k].rearrange("p e h -> p (e h)").bitcast(F32), ALU.subtract).then_inc(w_split, 1)

        @block.gpsimd
        def _(pool):
            nc.gpsimd.memset(half_neg[:], -0.5).then_inc(const_set, 1)
            nc.gpsimd.memset(minus_mean[:], -1.0 / 128).then_inc(const_set, 1)
            nc.gpsimd.memset(feat[:], 0.0).then_inc(const_set, 1)
            for k, value in CONSTANTS.items():
                nc.gpsimd.memset(const[:, k], value).then_inc(const_set, 1)
            pool.wait_ge(const_set, 3 + len(CONSTANTS))

            steps = [0]

            def bn(ins):
                steps[0] += 1
                ins.then_inc(bn_step, 1)
                pool.wait_ge(bn_step, steps[0])

            pool.wait_ge(expert_w, 8 * 16)
            for k, (g, v, b, m, be, s, t) in enumerate(((G1, V1, B1, M1, BE1, S1, T1), (G2, V2, B2, M2, BE2, S2, T2))):
                bn(nc.gpsimd.tensor_scalar(bn_std[:, k], small_sb[:, v], BN_EPS, None, ALU.add))
                bn(nc.gpsimd.tensor_tensor(bn_tmp[:, k], bn_std[:, k], half_neg[0:EXPERTS, :], ALU.pow))
                bn(nc.gpsimd.tensor_tensor(rows[:, s], bn_tmp[:, k], small_sb[:, g], ALU.mult))
                bn(nc.gpsimd.tensor_tensor(bn_std[:, k], small_sb[:, b], small_sb[:, m], ALU.subtract))
                bn(nc.gpsimd.tensor_tensor(bn_tmp[:, k], bn_std[:, k], rows[:, s], ALU.mult))
                bn(nc.gpsimd.tensor_tensor(bn_std[:, k], bn_tmp[:, k], small_sb[:, be], ALU.add))
                bn(nc.gpsimd.tensor_scalar(rows[:, t], bn_std[:, k], 1.0 / 128 if k == 0 else 1.0, None, ALU.mult))
            nc.gpsimd.tensor_copy(bn_tmp[:], bn_std[:]).then_inc(rows_done, 1)

            def statistics(k, base, eps, done):
                s, o = st[k], ln[k]
                n = 0

                def then(ins):
                    nonlocal n
                    n += 1
                    ins.then_inc(ln_step, 1)

                def ready(count):
                    pool.wait_ge(ln_step, base + count)

                then(nc.gpsimd.tensor_tensor(o[:, 0], s[:, :, 1], s[:, :, 4], ALU.add))
                then(nc.gpsimd.tensor_tensor(o[:, 1], s[:, :, 1], s[:, :, 4], ALU.subtract))
                then(nc.gpsimd.tensor_tensor(o[:, 2], s[:, :, 2], s[:, :, 5], ALU.add))
                ready(2)
                then(nc.gpsimd.tensor_tensor(o[:, 3], o[:, 1], o[:, 1], ALU.mult))
                ready(4)
                then(nc.gpsimd.tensor_tensor(o[:, 4], o[:, 3], const[:, QUARTER_C], ALU.mult))
                ready(5)
                then(nc.gpsimd.tensor_tensor(o[:, 5], o[:, 4], o[:, 2], ALU.add))
                ready(6)
                then(nc.gpsimd.tensor_tensor(o[:, 3], o[:, 5], const[:, eps], ALU.add))
                ready(7)
                then(nc.gpsimd.tensor_tensor(o[:, 4], o[:, 3], const[:, MINUS_HALF], ALU.pow))
                ready(8)
                then(nc.gpsimd.tensor_tensor(o[:, 6], o[:, 4], const[:, ROOT_C], ALU.mult))
                ready(9)
                then(nc.gpsimd.tensor_tensor(o[:, 5], o[:, 0], o[:, 6], ALU.mult))
                ready(10)
                nc.gpsimd.tensor_tensor(o[:, 7], o[:, 5], const[:, MINUS_HALF], ALU.mult).then_inc(done, 1)
                assert n == LN_STEPS

            def step(t, p, a, b, c, d):
                before = LN_STEPS * (min(max(t + 1, 0), IMAGES) + min(max(t - 1, 0), IMAGES)) if isinstance(t, int) else 2 * LN_STEPS * t
                if a:
                    pool.wait_ge(stats1_done, t + 2)
                    wait(pool, norm1_done, t + 1)
                    statistics(0, before, LN_C_EPS_C, ln1_done)
                if c:
                    pool.wait_ge(stats2_done, t)
                    wait(pool, norm2_done, t - 1)
                    statistics(1, before + (LN_STEPS if a else 0), LN_T_EPS_C, ln2_done)
                    pool.wait_ge(norm2_done, t)
                    wait(pool, feat_done, t - 1)
                    nc.gpsimd.tensor_tensor(feat[:], feat[:], xn2T[:], ALU.add).then_inc(feat_done, 1)

            rounds(pool, step)


def expert_block(nc, banks, x1_dram, xn2_dram, w_hi, w_lo, ident, t2, bo_sb, wr_sb, br_sb, feat, out):
    SLOTS = IMAGES * EXPERTS
    L2_LAG, L3_LAG = 1, 3
    with ExitStack() as ctx:
        def sb(name, shape, dt=F32):
            return ctx.enter_context(nc.sbuf_tensor(name, shape, dt))

        def sem(name):
            return ctx.enter_context(nc.semaphore(name))

        featT = sb("featT", [C, PIXELS])
        logits = sb("logits", [128, CHUNKS, EXPERTS])
        top = sb("top", [128, CHUNKS])
        shifted = sb("shifted", [128, CHUNKS, EXPERTS])
        grown = sb("grown", [128, CHUNKS, EXPERTS])
        total = sb("total", [128, CHUNKS])
        share = sb("share", [128, CHUNKS])
        route = sb("route", [128, CHUNKS, EXPERTS])
        routeT = sb("routeT", [EXPERTS, PIXELS])
        route_all = sb("route_all", [128, EXPERTS, PIXELS])
        bias_out = sb("bias_out", [C, PIXELS])
        xn2 = [sb(f"b_xn2_{p}", [C, PIXELS]) for p in range(2)]
        x1 = [sb(f"b_x1_{p}", [C, PIXELS]) for p in range(2)]
        xs_hi = [sb(f"xs_hi{p}", [C, PIXELS], F32R) for p in range(2)]
        xs_lo = [sb(f"xs_lo{p}", [C, PIXELS], F32R) for p in range(2)]
        h1_hi = [sb(f"h1_hi{p}", [HIDDEN, PIXELS], F32R) for p in range(2)]
        h1_lo = [sb(f"h1_lo{p}", [HIDDEN, PIXELS], F32R) for p in range(2)]
        h2 = [sb(f"h2_{p}", [HIDDEN, PIXELS]) for p in range(2)]
        h2w = [sb(f"h2w_{p}", [HIDDEN, PIXELS]) for p in range(2)]
        h2_hi = [sb(f"h2_hi{p}", [HIDDEN, PIXELS], F32R) for p in range(2)]
        h2_lo = [sb(f"h2_lo{p}", [HIDDEN, PIXELS], F32R) for p in range(2)]

        z1, z2, y = [banks(0, 2), banks(2, 2)], banks(4, 2), banks(6, 2)

        xn2_loaded = [sem(f"xn2_loaded{p}") for p in range(2)]
        x1_loaded = [sem(f"x1_loaded{p}") for p in range(2)]
        out_stored = [sem(f"out_stored{p}") for p in range(2)]
        turned, feat_moved, logits_done, step_done = sem("turned"), sem("feat_moved"), sem("logits_done"), sem("step_done")
        grown_done, route_done, routeT_done, routeT_moved = sem("grown_done"), sem("route_done"), sem("routeT_done"), sem("routeT_moved")
        spread, spread_moved_act, spread_moved_dve = sem("spread"), sem("spread_moved_act"), sem("spread_moved_dve")
        bias_done, bias_moved = sem("bias_done"), sem("bias_moved")
        l1_done, l2_done, l3_done = sem("l1_done"), sem("l2_done"), sem("l3_done")
        h1_hi_done, h1_lo_done, h2_done = sem("h1_hi_done"), sem("h1_lo_done"), sem("h2_done")
        h2w_done, h2_hi_done, h2_lo_done = sem("h2w_done"), sem("h2_hi_done"), sem("h2_lo_done")
        xs_hi_done, xs_lo_done, x1_biased, out_done = sem("xs_hi_done"), sem("xs_lo_done"), sem("x1_biased"), sem("out_done")

        def slots(engine, slot):
            period = 2 * EXPERTS
            first = L3_LAG + EXPERTS
            for s in range(first):
                slot(s, s, s // EXPERTS)
            trips = (SLOTS - first) // period
            with engine.Fori(0, trips) as i:
                for k in range(first, first + period):
                    slot(period * i + k, k % period, 2 * i + k // EXPERTS)
            for s in range(first + trips * period, SLOTS + L3_LAG):
                slot(s, s % period, s // EXPERTS)

        def exists(s):
            return not isinstance(s, int) or 0 <= s < SLOTS

        block = ctx.enter_context(nc.Block())

        @block.sync
        def _(sp):
            def load(b, p, inside):
                if inside:
                    sp.wait_ge(xs_lo_done, b - 1)
                    sp.wait_ge(xs_hi_done, b - 1)
                sp.dma_start(xn2[p][:], xn2_dram[b]).then_inc(xn2_loaded[p], 16)
                if inside:
                    sp.wait_ge(out_done, b - 1)
                    sp.dma_start(out[b - 2], x1[p][:]).then_inc(out_stored[p], 16)
                    sp.wait_ge(out_stored[p], 8 * b - 8 * p)
                sp.dma_start(x1[p][:], x1_dram[b]).then_inc(x1_loaded[p], 16)

            load(0, 0, False)
            load(1, 1, False)
            with sp.Fori(0, IMAGES // 2 - 1) as i:
                for p in range(2):
                    load(2 * i + (2 + p), p, True)
            for p in range(2):
                sp.wait_ge(out_done, IMAGES - 1 + p)
                sp.dma_start(out[IMAGES - 2 + p], x1[p][:]).then_inc(out_stored[p], 16)
            for p in range(2):
                sp.wait_ge(out_stored[p], 16 * (IMAGES // 2))

        @block.tensor
        def _(pe):
            for n in range(CHUNKS):
                mm = pe.transpose(y[:, 128 * n:128 * (n + 1)], feat[:, n, :], ident[:])
            mm.then_inc(turned, 1)
            pe.wait_ge(feat_moved, 1)
            for n in range(CHUNKS):
                mm = pe.matmul(z2[:, EXPERTS * n:EXPERTS * (n + 1)], featT[:, 128 * n:128 * (n + 1)], wr_sb[:], start=True, stop=True)
            mm.then_inc(logits_done, 1)
            pe.wait_ge(route_done, 1)
            for n in range(CHUNKS):
                mm = pe.transpose(y[0:EXPERTS, 128 * n:128 * (n + 1)], route[:, n, :], ident[:])
            mm.then_inc(routeT_done, 1)
            for e in range(EXPERTS):
                if e >= 2:
                    pe.wait_ge((spread_moved_act, spread_moved_dve)[e % 2], e // 2)
                for n in range(CHUNKS):
                    mm = pe.transpose(z1[e % 2][:, 128 * n:128 * (n + 1)],
                                      route[:, n, e:e + 1].to_broadcast([128, 128]), ident[:])
                mm.then_inc(spread, 1)
            pe.wait_ge(routeT_moved, 1)
            for n in range(2):
                mm = pe.matmul(z2[:, BANK * n:BANK * (n + 1)], bo_sb[:], routeT[:, BANK * n:BANK * (n + 1)], start=True, stop=True)
            mm.then_inc(bias_done, 1)
            pe.wait_ge(spread_moved_act, EXPERTS // 2)
            pe.wait_ge(spread_moved_dve, EXPERTS // 2)
            pe.wait_ge(bias_moved, 1)

            def layer(dst, which, e, hi, lo, first, last):
                for w, part in ((w_hi, hi), (w_lo, hi), (w_hi, lo)):
                    for n in range(2):
                        cols = slice(BANK * n, BANK * (n + 1))
                        mm = pe.matmul(dst[:, cols], w[:, which, e, :], part[:, cols],
                                       start=first and w is w_hi and part is hi, stop=last and part is lo, skip_group_check=True)
                return mm

            def slot(s, k, image):
                if exists(s):
                    e, p = k % EXPERTS, k // EXPERTS
                    if e == 0:
                        pe.wait_ge(xs_lo_done, image + 1)
                    wait(pe, h1_lo_done, s - 1)
                    layer(z1[k % 2], 0, e, xs_hi[p], xs_lo[p], True, True).then_inc(l1_done, 1)
                if exists(s - L2_LAG):
                    pe.wait_ge(h1_lo_done, s - L2_LAG + 1)
                    wait(pe, h2_done, s - L2_LAG)
                    r = (k - L2_LAG) % 2
                    layer(z2, 1, (k - L2_LAG) % EXPERTS, h1_hi[r], h1_lo[r], True, True).then_inc(l2_done, 1)
                if exists(s - L3_LAG):
                    e = (k - L3_LAG) % EXPERTS
                    pe.wait_ge(h2_lo_done, s - L3_LAG + 1)
                    if e == 0:
                        wait(pe, out_done, image)
                    r = (k - L3_LAG) % 2
                    layer(y, 2, e, h2_hi[r], h2_lo[r], e == 0, e == EXPERTS - 1).then_inc(l3_done, 1)

            slots(pe, slot)

        @block.scalar
        def _(act):
            act.wait_ge(turned, 1)
            nc.scalar.mul(featT[:], y, 1.0 / IMAGES).then_inc(feat_moved, 1)
            act.wait_ge(xn2_loaded[0], 16)
            nc.scalar.copy(xs_hi[0][:], xn2[0][:]).then_inc(xs_hi_done, 1)
            act.wait_ge(step_done, 3)
            nc.scalar.activation(grown[:].rearrange("p n e -> p (n e)"), shifted[:].rearrange("p n e -> p (n e)"), ACT.Exp).then_inc(grown_done, 1)
            act.wait_ge(routeT_done, 1)
            nc.scalar.copy(routeT[:], y[0:EXPERTS, :]).then_inc(routeT_moved, 1)
            for e in range(0, EXPERTS, 2):
                act.wait_ge(spread, e + 1)
                nc.scalar.copy(route_all[:, e, :], z1[0]).then_inc(spread_moved_act, 1)
            act.wait_ge(bias_done, 1)
            nc.scalar.copy(bias_out[:], z2).then_inc(bias_moved, 1)

            def slot(s, k, image):
                if exists(s - 2):
                    r = k % 2
                    act.wait_ge(h2w_done, s - 1)
                    wait(act, l3_done, s - 3)
                    nc.scalar.copy(h2_hi[r][:], h2w[r][:]).then_inc(h2_hi_done, 1)
                if exists(s):
                    r = k % 2
                    act.wait_ge(l1_done, s + 1)
                    wait(act, l2_done, s - 1)
                    nc.scalar.activation(h1_hi[r][:], z1[r], ACT.Relu).then_inc(h1_hi_done, 1)
                if exists(s - 1):
                    r, e = (k - 1) % 2, (k - 1) % EXPERTS
                    act.wait_ge(l2_done, s)
                    wait(act, h2w_done, s - 2)
                    nc.scalar.activation(h2[r][:], z2, ACT.Relu, bias=t2[:, e:e + 1]).then_inc(h2_done, 1)
                if k % EXPERTS == 5 and exists(s + EXPERTS):
                    p = 1 - k // EXPERTS
                    act.wait_ge(xn2_loaded[p], 8 * image + (16 if p else 24))
                    wait(act, l1_done, s - 5)
                    nc.scalar.copy(xs_hi[p][:], xn2[p][:]).then_inc(xs_hi_done, 1)

            slots(act, slot)

        @block.vector
        def _(dve):
            dve.wait_ge(xs_hi_done, 1)
            nc.vector.tensor_tensor(xs_lo[0][:], xn2[0][:], xs_hi[0][:].bitcast(F32), ALU.subtract).then_inc(xs_lo_done, 1)
            dve.wait_ge(logits_done, 1)
            nc.vector.tensor_tensor(logits[:], z2[:, 0:CHUNKS * EXPERTS].rearrange("p (n e) -> p n e", e=EXPERTS),
                                    br_sb[:].unsqueeze(1).to_broadcast([128, CHUNKS, EXPERTS]), ALU.add).then_inc(step_done, 1)
            dve.wait_ge(step_done, 1)
            nc.vector.tensor_reduce(top[:], logits[:], AX.X, ALU.max).then_inc(step_done, 1)
            dve.wait_ge(step_done, 2)
            nc.vector.tensor_tensor(shifted[:], logits[:], top[:].unsqueeze(2).to_broadcast([128, CHUNKS, EXPERTS]),
                                    ALU.subtract).then_inc(step_done, 1)
            dve.wait_ge(grown_done, 1)
            nc.vector.tensor_reduce(total[:], grown[:], AX.X, ALU.add).then_inc(step_done, 1)
            dve.wait_ge(step_done, 4)
            nc.vector.reciprocal(share[:], total[:]).then_inc(step_done, 1)
            dve.wait_ge(step_done, 5)
            nc.vector.tensor_tensor(route[:], grown[:], share[:].unsqueeze(2).to_broadcast([128, CHUNKS, EXPERTS]),
                                    ALU.mult).then_inc(route_done, 1)
            for e in range(1, EXPERTS, 2):
                dve.wait_ge(spread, e + 1)
                nc.vector.tensor_copy(route_all[:, e, :], z1[1]).then_inc(spread_moved_dve, 1)
            dve.wait_ge(spread_moved_act, EXPERTS // 2)

            def slot(s, k, image):
                if exists(s - 2):
                    r = k % 2
                    dve.wait_ge(h2_hi_done, s - 1)
                    nc.vector.tensor_tensor(h2_lo[r][:], h2w[r][:], h2_hi[r][:].bitcast(F32), ALU.subtract).then_inc(h2_lo_done, 1)
                if exists(s):
                    r = k % 2
                    dve.wait_ge(h1_hi_done, s + 1)
                    nc.vector.scalar_tensor_tensor(out=h1_lo[r][:], in0=z1[r], scalar=0.0, in1=h1_hi[r][:].bitcast(F32),
                                                   op0=ALU.max, op1=ALU.subtract).then_inc(h1_lo_done, 1)
                if exists(s - 1):
                    r, e = (k - 1) % 2, (k - 1) % EXPERTS
                    dve.wait_ge(h2_done, s)
                    wait(dve, h2_hi_done, s - 2)
                    wait(dve, h2_lo_done, s - 2)
                    nc.vector.tensor_tensor(h2w[r][:], h2[r][:], route_all[:, e, :], ALU.mult).then_inc(h2w_done, 1)
                if k % EXPERTS == 5 and exists(s + EXPERTS):
                    p = 1 - k // EXPERTS
                    dve.wait_ge(xs_hi_done, image + 2)
                    nc.vector.tensor_tensor(xs_lo[p][:], xn2[p][:], xs_hi[p][:].bitcast(F32), ALU.subtract).then_inc(xs_lo_done, 1)
                if k % EXPERTS == 2 and exists(s - EXPERTS):
                    p = 1 - k // EXPERTS
                    dve.wait_ge(l3_done, s - 2)
                    dve.wait_ge(x1_biased, image)
                    nc.vector.tensor_tensor(x1[p][:], y, x1[p][:], ALU.add).then_inc(out_done, 1)

            slots(dve, slot)

        @block.gpsimd
        def _(pool):
            pool.wait_ge(bias_moved, 1)
            with pool.Fori(0, IMAGES // 2) as i:
                for p in range(2):
                    pool.wait_ge(x1_loaded[p], 16 * i + 16)
                    nc.gpsimd.tensor_tensor(x1[p][:], x1[p][:], bias_out[:], ALU.add).then_inc(x1_biased, 1)




def kernel(x, L0_conv_w_qkv, L0_conv_w_out, L0_conv_b_out, L0_ffn_Wr, L0_ffn_br, L0_ffn_W1, L0_ffn_b1, L0_ffn_g1,
           L0_ffn_be1, L0_ffn_m1, L0_ffn_v1, L0_ffn_W2, L0_ffn_b2, L0_ffn_g2, L0_ffn_be2, L0_ffn_m2, L0_ffn_v2,
           L0_ffn_Wo, L0_ffn_bo):
    import concourse.bacc as bacc
    from concourse.bass_utils import run_bass_kernel_spmd as run

    small = np.stack([np.asarray(a) for a in (
        L0_ffn_g1, L0_ffn_v1, L0_ffn_b1, L0_ffn_m1, L0_ffn_be1,
        L0_ffn_g2, L0_ffn_v2, L0_ffn_b2, L0_ffn_m2, L0_ffn_be2)], axis=1)
    arrays = {
        "x": np.asarray(x).reshape(IMAGES, C, PIXELS),
        "w_qkv": np.asarray(L0_conv_w_qkv),
        "w_out": np.asarray(L0_conv_w_out),
        "b_out": np.asarray(L0_conv_b_out).reshape(C, 1),
        "Wr": np.asarray(L0_ffn_Wr),
        "br": np.ascontiguousarray(np.broadcast_to(np.asarray(L0_ffn_br)[None, :], (128, EXPERTS))),
        "W1": np.asarray(L0_ffn_W1),
        "W2": np.asarray(L0_ffn_W2),
        "Wo": np.asarray(L0_ffn_Wo),
        "small": np.ascontiguousarray(small),
        "bo": np.asarray(L0_ffn_bo),
        "ident": np.eye(128, dtype=np.float32),
        "heads": np.kron(np.eye(128 // HEAD_DIM), np.ones((HEAD_DIM, HEAD_DIM))).astype(np.float32),
        "sel": np.repeat(np.eye(EXPERTS, dtype=np.float32)[:, :, None], 128, axis=2),
    }
    nc = bacc.Bacc("TRN2", target_bir_lowering=False, num_devices=1)
    arrays = {f"in_{name}": np.ascontiguousarray(a) for name, a in arrays.items()}
    args = [nc.dram_tensor(name, a.shape, F32, kind="ExternalInput").ap() for name, a in arrays.items()]
    out = nc.dram_tensor("out_0", [IMAGES, C, PIXELS], F32, kind="ExternalOutput").ap()
    metaformer_kernel(nc, *args, out)
    result = run(nc, [arrays], core_ids=[0]).results[0]["out_0"]
    return result.reshape(IMAGES, C, SIDE, SIDE)
```

```python
from contextlib import ExitStack

import numpy as np

import concourse.bass as bass
from concourse import mybir

F32 = mybir.dt.float32
F32R = mybir.dt.float32r
ALU = mybir.AluOpType
ACT = mybir.ActivationFunctionType
AX = mybir.AxisListType

IMAGES, C, SIDE = 16, 128, 32
PIXELS = SIDE * SIDE
CHUNKS = PIXELS // 128
HEADS, HEAD_DIM = 8, 32
LATENT = HEADS * HEAD_DIM
EXPERTS, HIDDEN = 8, 128
BANK = 512
LN_C_EPS, LN_T_EPS, BN_EPS = 1e-6, 1e-5, 1e-3
G1, V1, B1, M1, BE1, G2, V2, B2, M2, BE2 = range(10)
S1, T1, S2 = range(3)
QUARTER_C, ROOT_C, MINUS_HALF, LN_C_EPS_C, LN_T_EPS_C, BN_EPS_K, ONE_C = range(7)
CONSTANTS = {QUARTER_C: C / 4, ROOT_C: C ** 0.5, MINUS_HALF: -0.5, LN_C_EPS_C: C * LN_C_EPS, LN_T_EPS_C: C * LN_T_EPS,
             BN_EPS_K: BN_EPS, ONE_C: 1.0 / C}


def wait(engine, semaphore, count):
    if not isinstance(count, int) or count > 0:
        engine.wait_ge(semaphore, count)


def metaformer_kernel(nc, x, w_qkv, w_out, b_out, Wr, br, W1, W2, Wo, small, bo, ident_in, heads_in, out):
    x1_dram = nc.dram_tensor("x1_scratch", [IMAGES, C, PIXELS], F32, kind="Internal").ap()
    xn2_dram = nc.dram_tensor("xn2_scratch", [IMAGES, C, PIXELS], F32, kind="Internal").ap()

    with ExitStack() as whole:
        def keep(name, shape, dt=F32):
            return whole.enter_context(nc.sbuf_tensor(name, shape, dt))

        psum = whole.enter_context(nc.psum_tensor("psum", [128, 8, BANK], F32))

        def banks(first, n):
            return psum[:, first:first + n, :].rearrange("p b n -> p (b n)")

        w_hi = keep("w_hi", [128, 3, EXPERTS, 128], F32R)
        w_lo = keep("w_lo", [128, 3, EXPERTS, 128], F32R)
        ident = keep("ident", [128, 128])
        t2 = keep("t2", [HIDDEN, EXPERTS])
        bo_sb = keep("bo_sb", [EXPERTS, C])
        wr_sb = keep("wr_sb", [C, EXPERTS])
        br_sb = keep("br_sb", [128, EXPERTS])
        feat = keep("feat", [128, CHUNKS, C])

        attention_block(nc, psum, banks, x, w_qkv, w_out, b_out, Wr, br, W1, W2, Wo, small, bo,
                        ident_in, heads_in, x1_dram, xn2_dram,
                        w_hi, w_lo, ident, t2, bo_sb, wr_sb, br_sb, feat)
        expert_block(nc, banks, x1_dram, xn2_dram, w_hi, w_lo, ident, t2, bo_sb, wr_sb, br_sb, feat, out)


def attention_block(nc, psum, banks, x, w_qkv, w_out, b_out, Wr, br, W1, W2, Wo, small, bo,
                    ident_in, heads_in, x1_dram, xn2_dram,
                    w_hi, w_lo, ident, t2, bo_sb, wr_sb, br_sb, feat):
    with ExitStack() as ctx:
        def sb(name, shape, dt=F32):
            return ctx.enter_context(nc.sbuf_tensor(name, shape, dt))

        def sem(name):
            return ctx.enter_context(nc.semaphore(name))

        heads = sb("heads", [128, 128])
        wqkv_sb = sb("wqkv_sb", [128, 6, C])
        wout_sb = sb("wout_sb", [C, LATENT])
        bout_sb = sb("bout_sb", [C, 1])
        wkT_hi = sb("wkT_hi", [C, LATENT], F32R)
        wkT_lo = sb("wkT_lo", [C, LATENT], F32R)
        wvT = sb("wvT", [C, LATENT])
        woutT = sb("woutT", [128, 2, C])
        w_raw = sb("w_raw", [128, 3, EXPERTS, 128])
        small_sb = sb("small_sb", [HIDDEN, 10, EXPERTS])
        bn_std = sb("bn_std", [HIDDEN, 2, EXPERTS])
        bn_tmp = sb("bn_tmp", [HIDDEN, 2, EXPERTS])
        cols = sb("cols", [HIDDEN, 3, EXPERTS])
        minus_mean = sb("minus_mean", [128, 128])
        xT = sb("xT", [128, CHUNKS, C])
        x1T = [sb(f"x1T{p}", [128, CHUNKS, C]) for p in range(2)]
        ln_wait = sb("ln_wait", [128, CHUNKS])
        const = sb("const", [128, len(CONSTANTS), CHUNKS])
        x_in = [sb(f"x_in{p}", [C, PIXELS]) for p in range(2)]
        x_res = [sb(f"x_res{p}", [C, PIXELS]) for p in range(2)]
        xnT = [sb(f"xnT{p}", [128, CHUNKS, C]) for p in range(2)]
        xn_hi = [sb(f"xn_hi{p}", [C, PIXELS], F32R) for p in range(2)]
        xn_lo = [sb(f"xn_lo{p}", [C, PIXELS], F32R) for p in range(2)]
        ek = [sb(f"ek{j}", [128, PIXELS]) for j in range(2)]
        ekT = [sb(f"ekT{j}", [128, CHUNKS, 128]) for j in range(2)]
        negmax = sb("negmax", [128, 2])
        rawmax = sb("rawmax", [128, 2])
        sums = [sb(f"sums{p}", [128, 2]) for p in range(2)]
        rsum = sb("rsum", [128, 2])
        gT = sb("gT", [C, LATENT])
        ctxT = sb("ctxT", [128, 2, 128])
        y_sb = sb("y_sb", [128, 2, C])
        mT_hi = sb("mT_hi", [C, C], F32R)
        mT_lo = sb("mT_lo", [C, C], F32R)
        xn2T = sb("xn2T", [128, CHUNKS, C])
        xn2 = [sb(f"xn2_{p}", [C, PIXELS]) for p in range(2)]
        st = [sb(f"st{k}", [128, CHUNKS, 6]) for k in range(2)]
        ln = [sb(f"ln{k}", [128, 8, CHUNKS]) for k in range(2)]

        p_tok, p_chan, p_k, p_e, p_g = banks(0, 2), banks(2, 2), banks(4, 2), banks(6, 1), banks(7, 1)

        attn_w = sem("attn_w")
        expert_w = sem("expert_w")
        in_loaded = [sem(f"in_loaded{p}") for p in range(2)]
        res_loaded = [sem(f"res_loaded{p}") for p in range(2)]
        x1_stored = [sem(f"x1_stored{p}") for p in range(2)]
        xn2_stored = [sem(f"xn2_stored{p}") for p in range(2)]
        const_set = sem("const_set")
        wT_done, wk_hi_done, wT_moved = sem("wT_done"), sem("wk_hi_done"), sem("wT_moved")
        bn_step, cols_done, bcast_done, scaled = sem("bn_step"), sem("cols_done"), sem("bcast_done"), sem("scaled")
        shift_done, w1_shifted, w_hi_done, w_split = sem("shift_done"), sem("w1_shifted"), sem("w_hi_done"), sem("w_split")
        k_done, ctx_done, tx_done, y_done = sem("k_done"), sem("ctx_done"), sem("tx_done"), sem("y_done")
        m_done, mx_done, e_done, g_done = sem("m_done"), sem("mx_done"), sem("e_done"), sem("g_done")
        xnt_done, x1t_done, xn2t_done = sem("xnt_done"), sem("x1t_done"), sem("xn2t_done")
        xn2_moved, exp_done, m_hi_done, norm1_done = sem("xn2_moved"), sem("exp_done"), sem("m_hi_done"), sem("norm1_done")
        e_moved, xn_hi_done, norm2_done = sem("e_moved"), sem("xn_hi_done"), sem("norm2_done")
        copy1_done, copy2_done = sem("copy1_done"), sem("copy2_done")
        g_moved, max_done, negmax_done, ctx_moved = sem("g_moved"), sem("max_done"), sem("negmax_done"), sem("ctx_moved")
        rsum_done, y_moved, stats1_done, m_lo_done = sem("rsum_done"), sem("y_moved"), sem("stats1_done"), sem("m_lo_done")
        x1_done, xn_lo_done, stats2_done = sem("x1_done"), sem("xn_lo_done"), sem("stats2_done")
        ln_step, ln1_done, ln2_done, feat_done = sem("ln_step"), sem("ln1_done"), sem("ln2_done"), sem("feat_done")

        LN_STEPS = 10

        def rounds(engine, step):
            def valid(t):
                return dict(a=t + 1 < IMAGES, b=0 <= t < IMAGES, c=0 <= t - 1 < IMAGES, f=0 <= t - 2 < IMAGES,
                            d=0 <= t - 3 < IMAGES)
            for t in range(-1, 6):
                step(t, t % 2, **valid(t))
            with engine.Fori(0, (IMAGES - 8) // 2) as i:
                for p in range(2):
                    step(2 * i + (6 + p), p, a=True, b=True, c=True, f=True, d=True)
            for t in range(IMAGES - 2, IMAGES + 3):
                step(t, t % 2, **valid(t))

        block = ctx.enter_context(nc.Block())

        @block.sync
        def _(sp):
            sp.dma_start(ident[:], ident_in).then_inc(attn_w, 16)
            sp.dma_start(x_in[0][:], x[0]).then_inc(in_loaded[0], 16)
            sp.dma_start(wqkv_sb[:], w_qkv.rearrange("(t p) c -> p t c", p=128)).then_inc(attn_w, 16)
            sp.dma_start(wout_sb[:], w_out).then_inc(attn_w, 16)
            sp.dma_start(heads[:], heads_in).then_inc(attn_w, 16)
            sp.dma_start(bout_sb[:], b_out).then_inc(attn_w, 16)
            sp.dma_start(x_in[1][:], x[1]).then_inc(in_loaded[1], 16)
            sp.dma_start(small_sb[:], small).then_inc(expert_w, 16)
            sp.dma_start(bo_sb[:], bo).then_inc(expert_w, 16)
            sp.dma_start(wr_sb[:], Wr).then_inc(expert_w, 16)
            sp.dma_start(br_sb[:], br).then_inc(expert_w, 16)
            for k, w in enumerate((W1, W2, Wo)):
                sp.dma_start(w_raw[:, k], w.rearrange("e c h -> c e h")).then_inc(expert_w, 16)

            def step(t, p, a, b, c, f, d):
                q = 1 - p
                if not isinstance(t, int) or 0 <= t < IMAGES - 2:
                    sp.wait_ge(tx_done, t + 1)
                    sp.dma_start(x_in[p][:], x[t + 2]).then_inc(in_loaded[p], 16)
                if b:
                    if not isinstance(t, int) or t >= 2:
                        sp.wait_ge(x1t_done, t - 1)
                        sp.wait_ge(x1_stored[p], 8 * t - 8 * p)
                    sp.dma_start(x_res[p][:], x[t]).then_inc(res_loaded[p], 16)
                if d:
                    sp.wait_ge(xn2_moved, t - 2)
                    sp.dma_start(xn2_dram[t - 3], xn2[q][:]).then_inc(xn2_stored[q], 16)
                if c:
                    sp.wait_ge(x1_done, t)
                    sp.dma_start(x1_dram[t - 1], x_res[q][:]).then_inc(x1_stored[q], 16)

            rounds(sp, step)
            for p in range(2):
                sp.wait_ge(x1_stored[p], 16 * (IMAGES // 2))
                sp.wait_ge(xn2_stored[p], 16 * (IMAGES // 2))

        @block.tensor
        def _(pe):
            pe.wait_ge(attn_w, 5 * 16)
            for k in range(4):
                pe.transpose(p_tok[:, 128 * k:128 * (k + 1)], wqkv_sb[:, 2 + k, :], ident[:])
            for j in range(2):
                mm = pe.transpose(p_tok[:, BANK + 128 * j:BANK + 128 * (j + 1)], wout_sb[:, 128 * j:128 * (j + 1)], ident[:])
            mm.then_inc(wT_done, 1)

            def step(t, p, a, b, c, f, d):
                q = 1 - p
                if a:
                    pe.wait_ge(in_loaded[q], 8 * t + (24 if p else 16))
                    if isinstance(t, int) and t == -1:
                        pe.wait_ge(wT_moved, 1)
                    wait(pe, copy2_done, t - 2)
                    turn(p_tok, lambda n: x_in[q][:, 128 * n:128 * (n + 1)]).then_inc(tx_done, 1)
                if c:
                    pe.wait_ge(g_moved, t)
                    for j in range(2):
                        half = slice(128 * j, 128 * (j + 1))
                        mm = pe.matmul(p_g[:, 256 + 128 * j:256 + 128 * (j + 1)], wvT[:, half], gT[:, half], start=True, stop=True)
                    mm.then_inc(ctx_done, 1)
                if f:
                    if a:
                        pe.wait_ge(copy1_done, t + 2)
                    else:
                        wait(pe, copy2_done, t - 2)
                    pe.wait_ge(x1_done, t - 1)
                    turn(p_tok, lambda n: x_res[p][:, 128 * n:128 * (n + 1)]).then_inc(x1t_done, 1)
                if c:
                    pe.wait_ge(ctx_moved, t)
                    for j in range(2):
                        mm = pe.matmul(p_g[:, 128 * j:128 * (j + 1)], ctxT[:, j, :], woutT[:, j, :], start=True, stop=True)
                    mm.then_inc(y_done, 1)
                if b:
                    k_half(t, p, 0)
                if c:
                    pe.wait_ge(y_moved, t)
                    for j in range(2):
                        mm = pe.matmul(p_g[:, 256:384], wqkv_sb[:, j, :], y_sb[:, j, :], start=j == 0, stop=j == 1)
                    mm.then_inc(m_done, 1)
                if c:
                    pe.wait_ge(m_lo_done, t)
                    if b:
                        pe.wait_ge(xn_lo_done, t + 1)
                    wait(pe, xn2_moved, t - 3)
                    for n in range(2):
                        cols_n = slice(BANK * n, BANK * (n + 1))
                        pe.matmul(p_chan[:, cols_n], mT_hi[:], xn_hi[q][:, cols_n], start=True, stop=False)
                        pe.matmul(p_chan[:, cols_n], mT_hi[:], xn_lo[q][:, cols_n], start=False, stop=False)
                        mm = pe.matmul(p_chan[:, cols_n], mT_lo[:], xn_hi[q][:, cols_n], start=False, stop=True)
                    mm.then_inc(mx_done, 1)
                if b:
                    turn_e(t, 0, 0)
                    k_half(t, p, 1)
                    turn_e(t, 0, 1)
                if d:
                    pe.wait_ge(norm2_done, t - 2)
                    wait(pe, xn2_moved, t - 3)
                    pe.wait_ge(x1_done, min(t, IMAGES) if isinstance(t, int) else t)
                    turn(p_chan, lambda n: xn2T[:, n, :]).then_inc(xn2t_done, 1)
                if b:
                    add_g(t, p, 0, 0)
                    add_g(t, p, 0, 1)
                    turn_e(t, 1, 0)
                if a:
                    pe.wait_ge(norm1_done, t + 2)
                    wait(pe, x1_done, t)
                    wait(pe, xn2_moved, t - 2)
                    turn(p_chan, lambda n: xnT[q][:, n, :]).then_inc(xnt_done, 1)
                if b:
                    turn_e(t, 1, 1)
                    add_g(t, p, 1, 0)
                    add_g(t, p, 1, 1)

            def turn(dst, chunk):
                for n in range(CHUNKS):
                    mm = pe.transpose(dst[:, 128 * n:128 * (n + 1)], chunk(n), ident[:])
                return mm

            def k_half(t, p, j):
                half = slice(128 * j, 128 * (j + 1))
                if j == 0:
                    pe.wait_ge(xn_lo_done, t + 1)
                wait(pe, exp_done, 2 * t + j)
                for w, xs in ((wkT_hi, xn_hi), (wkT_lo, xn_hi), (wkT_hi, xn_lo)):
                    for n in range(2):
                        cols = slice(BANK * n, BANK * (n + 1))
                        mm = pe.matmul(p_k[:, cols], w[:, half], xs[p][:, cols],
                                       start=w is wkT_hi and xs is xn_hi, stop=xs is xn_lo, skip_group_check=True)
                mm.then_inc(k_done, 1)

            def turn_e(t, j, h):
                if h == 0:
                    pe.wait_ge(exp_done, 2 * t + j + 1)
                wait(pe, e_moved, 4 * t + 2 * j + h)
                for n in range(4):
                    chunk = 4 * h + n
                    mm = pe.transpose(p_e[:, 128 * n:128 * (n + 1)], ek[j][:, 128 * chunk:128 * (chunk + 1)], ident[:])
                mm.then_inc(e_done, 1)

            def add_g(t, p, j, h):
                pe.wait_ge(e_moved, 4 * t + 2 * j + h + 1)
                for n in range(4):
                    chunk = 4 * h + n
                    mm = pe.matmul(p_g[:, 128 * j:128 * (j + 1)], xnT[p][:, chunk, :], ekT[j][:, chunk, :],
                                   start=chunk == 0, stop=chunk == CHUNKS - 1)
                if (j, h) == (1, 1):
                    mm.then_inc(g_done, 1)

            rounds(pe, step)

            pe.wait_ge(cols_done, 1)
            pe.wait_ge(expert_w, 7 * 16)
            pe.wait_ge(copy2_done, IMAGES)
            for dst, col in ((p_tok, S1), (p_k, S2)):
                for e in range(EXPERTS):
                    mm = pe.transpose(dst[:, 128 * e:128 * (e + 1)], cols[:, col, e:e + 1].to_broadcast([128, 128]), ident[:])
            mm.then_inc(bcast_done, 1)
            pe.wait_ge(scaled, 1)
            pe.wait_ge(xn2_moved, IMAGES)
            for e in range(EXPERTS):
                pe.matmul(p_chan[:, 128 * e:128 * (e + 1)], minus_mean[:], w_raw[:, 0, e, :], start=True, stop=False)
                mm = pe.matmul(p_chan[:, 128 * e:128 * (e + 1)], cols[:, T1, e:e + 1].to_broadcast([128, 128]), ident[:],
                               start=False, stop=True)
            mm.then_inc(shift_done, 1)

        @block.scalar
        def _(act):
            act.wait_ge(wT_done, 1)
            nc.scalar.copy(wkT_hi[:], p_tok[:, 0:LATENT]).then_inc(wk_hi_done, 1)

            def step(t, p, a, b, c, f, d):
                q = 1 - p
                if a:
                    act.wait_ge(tx_done, t + 2)
                    wait(act, norm1_done, t + 1)
                    nc.scalar.copy(xT[:], p_tok).then_inc(copy1_done, 1)
                if f:
                    act.wait_ge(x1t_done, t - 1)
                    wait(act, norm2_done, t - 3)
                    nc.scalar.copy(x1T[p][:], p_tok).then_inc(copy2_done, 1)
                if c:
                    act.wait_ge(m_done, t)
                    wait(act, mx_done, t - 1)
                    nc.scalar.copy(mT_hi[:], p_g[:, 256:384]).then_inc(m_hi_done, 1)
                if b:
                    exp_half(t, p, 0)
                    move_e(t, 0, 0)
                    move_e(t, 0, 1)
                    exp_half(t, p, 1)
                if d:
                    act.wait_ge(xn2t_done, t - 2)
                    if not isinstance(t, int) or t >= 5:
                        act.wait_ge(xn2_stored[q], 8 * t - 24 - 8 * q)
                    nc.scalar.activation(xn2[q][:], p_chan, ACT.Copy, bias=1.0).then_inc(xn2_moved, 1)
                if b:
                    move_e(t, 1, 0)
                if a:
                    act.wait_ge(xnt_done, t + 2)
                    wait(act, mx_done, t)
                    nc.scalar.copy(xn_hi[q][:], p_chan).then_inc(xn_hi_done, 1)
                if b:
                    move_e(t, 1, 1)

            def move_e(t, j, h):
                act.wait_ge(e_done, 4 * t + 2 * j + h + 1)
                wait(act, g_done, t)
                nc.scalar.copy(ekT[j][:, 4 * h:4 * h + 4, :].rearrange("p n d -> p (n d)"), p_e).then_inc(e_moved, 1)

            def exp_half(t, p, j):
                act.wait_ge(negmax_done, 2 * t + j + 1)
                wait(act, e_done, 4 * t + 2 * j - 2)
                if j == 0:
                    wait(act, rsum_done, t - 1)
                nc.scalar.activation(ek[j][:], p_k, ACT.Exp, bias=negmax[:, j:j + 1],
                                     accum_out=sums[p][:, j:j + 1]).then_inc(exp_done, 1)

            rounds(act, step)

            act.wait_ge(scaled, 2)
            for k in (2, 1, 0):
                if k == 0:
                    act.wait_ge(w1_shifted, 1)
                nc.scalar.copy(w_hi[:, k].rearrange("p e h -> p (e h)"),
                               w_raw[:, k].rearrange("p e h -> p (e h)")).then_inc(w_hi_done, 1)

        @block.vector
        def _(dve):
            dve.wait_ge(wk_hi_done, 1)
            nc.vector.tensor_tensor(wkT_lo[:], p_tok[:, 0:LATENT], wkT_hi[:].bitcast(F32), ALU.subtract)
            nc.vector.tensor_copy(wvT[:], p_tok[:, LATENT:2 * LATENT])
            nc.vector.tensor_copy(woutT[:].rearrange("p j c -> p (j c)"), p_tok[:, BANK:BANK + LATENT]).then_inc(wT_moved, 1)

            def step(t, p, a, b, c, f, d):
                q = 1 - p
                if c:
                    dve.wait_ge(g_done, t)
                    wait(dve, ctx_done, t - 1)
                    nc.vector.tensor_copy(gT[:], p_g[:, 0:LATENT]).then_inc(g_moved, 1)
                if c:
                    dve.wait_ge(ctx_done, t)
                    wait(dve, y_done, t - 1)
                    for j in range(2):
                        ins = nc.vector.tensor_tensor(ctxT[:, j, :], p_g[:, 256 + 128 * j:256 + 128 * (j + 1)], heads[:], ALU.mult)
                    ins.then_inc(ctx_moved, 1)
                if a:
                    dve.wait_ge(copy1_done, t + 2)
                    wait(dve, ln1_done, t + 1)
                    for n in range(CHUNKS):
                        ins = nc.vector.bn_stats(st[0][:, n, :], xT[:, n, :])
                    ins.then_inc(stats1_done, 1)
                if c:
                    dve.wait_ge(exp_done, 2 * t)
                    nc.vector.reciprocal(rsum[:], sums[q][:]).then_inc(rsum_done, 1)
                    dve.wait_ge(rsum_done, t)
                    dve.wait_ge(y_done, t)
                    wait(dve, m_done, t - 1)
                    for j in range(2):
                        ins = nc.vector.tensor_scalar(y_sb[:, j, :], p_g[:, 128 * j:128 * (j + 1)], rsum[:, j:j + 1], None, ALU.mult)
                    ins.then_inc(y_moved, 1)
                if b:
                    head_max(t, 0)
                if c:
                    dve.wait_ge(m_hi_done, t)
                    nc.vector.tensor_tensor(mT_lo[:], p_g[:, 256:384], mT_hi[:].bitcast(F32), ALU.subtract).then_inc(m_lo_done, 1)
                if d:
                    dve.wait_ge(ln2_done, t - 2)
                    wait(dve, xn2t_done, t - 3)
                    wait(dve, feat_done, t - 3)
                    for n in range(CHUNKS):
                        ins = nc.vector.tensor_scalar(xn2T[:, n, :], x1T[q][:, n, :], ln[1][:, 6, n:n + 1], ln[1][:, 7, n:n + 1],
                                                      ALU.mult, ALU.add)
                    ins.then_inc(norm2_done, 1)
                if c:
                    dve.wait_ge(mx_done, t)
                    dve.wait_ge(res_loaded[q], 8 * t + (0 if q else 8))
                    nc.vector.scalar_tensor_tensor(out=x_res[q][:], in0=p_chan, scalar=bout_sb[:, 0:1], in1=x_res[q][:],
                                                   op0=ALU.add, op1=ALU.add).then_inc(x1_done, 1)
                if b:
                    head_max(t, 1)
                if f:
                    dve.wait_ge(copy2_done, t - 1)
                    wait(dve, ln2_done, t - 2)
                    for n in range(CHUNKS):
                        ins = nc.vector.bn_stats(st[1][:, n, :], x1T[p][:, n, :])
                    ins.then_inc(stats2_done, 1)
                if a:
                    dve.wait_ge(xn_hi_done, t + 2)
                    nc.vector.tensor_tensor(xn_lo[q][:], p_chan, xn_hi[q][:].bitcast(F32), ALU.subtract).then_inc(xn_lo_done, 1)

            def head_max(t, j):
                dve.wait_ge(k_done, 2 * t + j + 1)
                wait(dve, exp_done, 2 * t + j - 1)
                nc.vector.tensor_reduce(rawmax[:, j:j + 1], p_k, AX.X, ALU.max).then_inc(max_done, 1)
                dve.wait_ge(max_done, 2 * t + j + 1)
                nc.vector.tensor_scalar(negmax[:, j:j + 1], rawmax[:, j:j + 1], -1.0, None, ALU.mult).then_inc(negmax_done, 1)

            rounds(dve, step)

            dve.wait_ge(bcast_done, 1)
            flat = [w_raw[:, k].rearrange("p e h -> p (e h)") for k in range(3)]
            nc.vector.tensor_tensor(flat[0], flat[0], p_tok, ALU.mult).then_inc(scaled, 1)
            nc.vector.tensor_tensor(flat[1], flat[1], p_k, ALU.mult).then_inc(scaled, 1)
            dve.wait_ge(shift_done, 1)
            dve.wait_ge(scaled, 2)
            nc.vector.tensor_tensor(flat[0], flat[0], p_chan, ALU.add).then_inc(w1_shifted, 1)
            for n, k in enumerate((2, 1, 0)):
                dve.wait_ge(w_hi_done, n + 1)
                if k == 0:
                    dve.wait_ge(w1_shifted, 1)
                nc.vector.tensor_tensor(w_lo[:, k].rearrange("p e h -> p (e h)"), flat[k],
                                        w_hi[:, k].rearrange("p e h -> p (e h)").bitcast(F32), ALU.subtract).then_inc(w_split, 1)

        @block.gpsimd
        def _(pool):
            nc.gpsimd.memset(minus_mean[:], -1.0 / 128).then_inc(const_set, 1)
            nc.gpsimd.memset(feat[:], 0.0).then_inc(const_set, 1)
            for k, value in CONSTANTS.items():
                nc.gpsimd.memset(const[:, k], value).then_inc(const_set, 1)
            pool.wait_ge(const_set, 2 + len(CONSTANTS))

            steps = [0]

            def bn(ins):
                steps[0] += 1
                ins.then_inc(bn_step, 1)
                pool.wait_ge(bn_step, steps[0])

            pool.wait_ge(expert_w, 7 * 16)
            for k, (g, v, b, m, be, s) in enumerate(((G1, V1, B1, M1, BE1, S1), (G2, V2, B2, M2, BE2, S2))):
                bn(nc.gpsimd.tensor_tensor(bn_std[:, k], small_sb[:, v], const[:, BN_EPS_K], ALU.add))
                bn(nc.gpsimd.tensor_tensor(bn_tmp[:, k], bn_std[:, k], const[:, MINUS_HALF], ALU.pow))
                bn(nc.gpsimd.tensor_tensor(cols[:, s], bn_tmp[:, k], small_sb[:, g], ALU.mult))
                bn(nc.gpsimd.tensor_tensor(bn_std[:, k], small_sb[:, b], small_sb[:, m], ALU.subtract))
                bn(nc.gpsimd.tensor_tensor(bn_tmp[:, k], bn_std[:, k], cols[:, s], ALU.mult))
                if k == 0:
                    bn(nc.gpsimd.tensor_tensor(bn_std[:, k], bn_tmp[:, k], small_sb[:, be], ALU.add))
                    bn(nc.gpsimd.tensor_tensor(cols[:, T1], bn_std[:, k], const[:, ONE_C], ALU.mult))
                else:
                    nc.gpsimd.tensor_tensor(t2[:], bn_tmp[:, k], small_sb[:, be], ALU.add).then_inc(cols_done, 1)

            def statistics(k, base, eps, done):
                s, o = st[k], ln[k]
                n = 0

                def then(ins):
                    nonlocal n
                    n += 1
                    ins.then_inc(ln_step, 1)

                def ready(count):
                    pool.wait_ge(ln_step, base + count)

                then(nc.gpsimd.tensor_tensor(o[:, 0], s[:, :, 1], s[:, :, 4], ALU.add))
                then(nc.gpsimd.tensor_tensor(o[:, 1], s[:, :, 1], s[:, :, 4], ALU.subtract))
                then(nc.gpsimd.tensor_tensor(o[:, 2], s[:, :, 2], s[:, :, 5], ALU.add))
                ready(2)
                then(nc.gpsimd.tensor_tensor(o[:, 3], o[:, 1], o[:, 1], ALU.mult))
                ready(4)
                then(nc.gpsimd.tensor_tensor(o[:, 4], o[:, 3], const[:, QUARTER_C], ALU.mult))
                ready(5)
                then(nc.gpsimd.tensor_tensor(o[:, 5], o[:, 4], o[:, 2], ALU.add))
                ready(6)
                then(nc.gpsimd.tensor_tensor(o[:, 3], o[:, 5], const[:, eps], ALU.add))
                ready(7)
                then(nc.gpsimd.tensor_tensor(o[:, 4], o[:, 3], const[:, MINUS_HALF], ALU.pow))
                ready(8)
                then(nc.gpsimd.tensor_tensor(o[:, 6], o[:, 4], const[:, ROOT_C], ALU.mult))
                ready(9)
                then(nc.gpsimd.tensor_tensor(o[:, 5], o[:, 0], o[:, 6], ALU.mult))
                ready(10)
                nc.gpsimd.tensor_tensor(o[:, 7], o[:, 5], const[:, MINUS_HALF], ALU.mult).then_inc(done, 1)
                assert n == LN_STEPS

            def step(t, p, a, b, c, f, d):
                q = 1 - p
                if isinstance(t, int):
                    before = LN_STEPS * (min(t + 1, IMAGES) + max(t - 2, 0))
                else:
                    before = 2 * LN_STEPS * t - LN_STEPS
                if a:
                    pool.wait_ge(stats1_done, t + 2)
                    wait(pool, norm1_done, t + 1)
                    statistics(0, before, LN_C_EPS_C, ln1_done)
                    pool.wait_ge(ln1_done, t + 2)
                    wait(pool, g_done, t)
                    nc.gpsimd.tensor_tensor(ln_wait[:], const[:, ONE_C], const[:, ONE_C], ALU.add)
                    for n in range(CHUNKS):
                        ins = nc.gpsimd.tensor_scalar(xnT[q][:, n, :], xT[:, n, :], ln[0][:, 6, n:n + 1], ln[0][:, 7, n:n + 1],
                                                      ALU.mult, ALU.add)
                    ins.then_inc(norm1_done, 1)
                if d:
                    pool.wait_ge(norm2_done, t - 2)
                    wait(pool, feat_done, t - 3)
                    nc.gpsimd.tensor_tensor(feat[:], feat[:], xn2T[:], ALU.add).then_inc(feat_done, 1)
                if f:
                    pool.wait_ge(stats2_done, t - 1)
                    wait(pool, norm2_done, t - 2)
                    statistics(1, before + (LN_STEPS if a else 0), LN_T_EPS_C, ln2_done)

            rounds(pool, step)


def expert_block(nc, banks, x1_dram, xn2_dram, w_hi, w_lo, ident, t2, bo_sb, wr_sb, br_sb, feat, out):
    SLOTS = IMAGES * EXPERTS
    L2_LAG, L3_LAG = 1, 3
    with ExitStack() as ctx:
        def sb(name, shape, dt=F32):
            return ctx.enter_context(nc.sbuf_tensor(name, shape, dt))

        def sem(name):
            return ctx.enter_context(nc.semaphore(name))

        featT = sb("featT", [C, PIXELS])
        logits = sb("logits", [128, CHUNKS, EXPERTS])
        top = sb("top", [128, CHUNKS])
        shifted = sb("shifted", [128, CHUNKS, EXPERTS])
        grown = sb("grown", [128, CHUNKS, EXPERTS])
        total = sb("total", [128, CHUNKS])
        share = sb("share", [128, CHUNKS])
        route = sb("route", [128, CHUNKS, EXPERTS])
        routeT = sb("routeT", [EXPERTS, PIXELS])
        route_all = sb("route_all", [128, EXPERTS, PIXELS])
        bias_out = sb("bias_out", [C, PIXELS])
        xn2 = [sb(f"b_xn2_{p}", [C, PIXELS]) for p in range(2)]
        x1 = [sb(f"b_x1_{p}", [C, PIXELS]) for p in range(2)]
        xs_hi = [sb(f"xs_hi{p}", [C, PIXELS], F32R) for p in range(2)]
        xs_lo = [sb(f"xs_lo{p}", [C, PIXELS], F32R) for p in range(2)]
        h1_hi = [sb(f"h1_hi{p}", [HIDDEN, PIXELS], F32R) for p in range(2)]
        h1_lo = [sb(f"h1_lo{p}", [HIDDEN, PIXELS], F32R) for p in range(2)]
        h2 = [sb(f"h2_{p}", [HIDDEN, PIXELS]) for p in range(2)]
        h2w = [sb(f"h2w_{p}", [HIDDEN, PIXELS]) for p in range(2)]
        h2_hi = [sb(f"h2_hi{p}", [HIDDEN, PIXELS], F32R) for p in range(2)]
        h2_lo = [sb(f"h2_lo{p}", [HIDDEN, PIXELS], F32R) for p in range(2)]

        z1, z2, y = [banks(0, 2), banks(2, 2)], banks(4, 2), banks(6, 2)

        xn2_loaded = [sem(f"xn2_loaded{p}") for p in range(2)]
        x1_loaded = [sem(f"x1_loaded{p}") for p in range(2)]
        out_stored = [sem(f"out_stored{p}") for p in range(2)]
        turned, feat_moved, logits_done, step_done = sem("turned"), sem("feat_moved"), sem("logits_done"), sem("step_done")
        grown_done, route_done, routeT_done, routeT_moved = sem("grown_done"), sem("route_done"), sem("routeT_done"), sem("routeT_moved")
        spread, spread_moved_act, spread_moved_dve = sem("spread"), sem("spread_moved_act"), sem("spread_moved_dve")
        bias_done, bias_moved = sem("bias_done"), sem("bias_moved")
        l1_done, l2_done, l3_done = sem("l1_done"), sem("l2_done"), sem("l3_done")
        h1_hi_done, h1_lo_done, h2_done = sem("h1_hi_done"), sem("h1_lo_done"), sem("h2_done")
        h2w_done, h2_hi_done, h2_lo_done = sem("h2w_done"), sem("h2_hi_done"), sem("h2_lo_done")
        xs_hi_done, xs_lo_done, x1_biased, out_done = sem("xs_hi_done"), sem("xs_lo_done"), sem("x1_biased"), sem("out_done")

        def slots(engine, slot):
            period = 2 * EXPERTS
            first = L3_LAG + EXPERTS
            for s in range(first):
                slot(s, s, s // EXPERTS)
            trips = (SLOTS - first) // period
            with engine.Fori(0, trips) as i:
                for k in range(first, first + period):
                    slot(period * i + k, k % period, 2 * i + k // EXPERTS)
            for s in range(first + trips * period, SLOTS + L3_LAG):
                slot(s, s % period, s // EXPERTS)

        def exists(s):
            return not isinstance(s, int) or 0 <= s < SLOTS

        block = ctx.enter_context(nc.Block())

        @block.sync
        def _(sp):
            def load(b, p, inside):
                if inside:
                    sp.wait_ge(xs_lo_done, b - 1)
                    sp.wait_ge(xs_hi_done, b - 1)
                sp.dma_start(xn2[p][:], xn2_dram[b]).then_inc(xn2_loaded[p], 16)
                if inside:
                    sp.wait_ge(out_done, b - 1)
                    sp.dma_start(out[b - 2], x1[p][:]).then_inc(out_stored[p], 16)
                    sp.wait_ge(out_stored[p], 8 * b - 8 * p)
                sp.dma_start(x1[p][:], x1_dram[b]).then_inc(x1_loaded[p], 16)

            load(0, 0, False)
            load(1, 1, False)
            with sp.Fori(0, IMAGES // 2 - 1) as i:
                for p in range(2):
                    load(2 * i + (2 + p), p, True)
            for p in range(2):
                sp.wait_ge(out_done, IMAGES - 1 + p)
                sp.dma_start(out[IMAGES - 2 + p], x1[p][:]).then_inc(out_stored[p], 16)
            for p in range(2):
                sp.wait_ge(out_stored[p], 16 * (IMAGES // 2))

        @block.tensor
        def _(pe):
            for n in range(CHUNKS):
                mm = pe.transpose(y[:, 128 * n:128 * (n + 1)], feat[:, n, :], ident[:])
            mm.then_inc(turned, 1)
            pe.wait_ge(feat_moved, 1)
            for n in range(CHUNKS):
                mm = pe.matmul(z2[:, EXPERTS * n:EXPERTS * (n + 1)], featT[:, 128 * n:128 * (n + 1)], wr_sb[:], start=True, stop=True)
            mm.then_inc(logits_done, 1)
            pe.wait_ge(route_done, 1)
            for n in range(CHUNKS):
                mm = pe.transpose(y[0:EXPERTS, 128 * n:128 * (n + 1)], route[:, n, :], ident[:])
            mm.then_inc(routeT_done, 1)
            for e in range(EXPERTS):
                if e >= 2:
                    pe.wait_ge((spread_moved_act, spread_moved_dve)[e % 2], e // 2)
                for n in range(CHUNKS):
                    mm = pe.transpose(z1[e % 2][:, 128 * n:128 * (n + 1)],
                                      route[:, n, e:e + 1].to_broadcast([128, 128]), ident[:])
                mm.then_inc(spread, 1)
            pe.wait_ge(routeT_moved, 1)
            for n in range(2):
                mm = pe.matmul(z2[:, BANK * n:BANK * (n + 1)], bo_sb[:], routeT[:, BANK * n:BANK * (n + 1)], start=True, stop=True)
            mm.then_inc(bias_done, 1)
            pe.wait_ge(spread_moved_act, EXPERTS // 2)
            pe.wait_ge(spread_moved_dve, EXPERTS // 2)
            pe.wait_ge(bias_moved, 1)

            def layer(dst, which, e, hi, lo, first, last):
                for w, part in ((w_hi, hi), (w_lo, hi), (w_hi, lo)):
                    for n in range(2):
                        cols = slice(BANK * n, BANK * (n + 1))
                        mm = pe.matmul(dst[:, cols], w[:, which, e, :], part[:, cols],
                                       start=first and w is w_hi and part is hi, stop=last and part is lo, skip_group_check=True)
                return mm

            def slot(s, k, image):
                if exists(s):
                    e, p = k % EXPERTS, k // EXPERTS
                    if e == 0:
                        pe.wait_ge(xs_lo_done, image + 1)
                    wait(pe, h1_lo_done, s - 1)
                    layer(z1[k % 2], 0, e, xs_hi[p], xs_lo[p], True, True).then_inc(l1_done, 1)
                if exists(s - L2_LAG):
                    pe.wait_ge(h1_lo_done, s - L2_LAG + 1)
                    wait(pe, h2_done, s - L2_LAG)
                    r = (k - L2_LAG) % 2
                    layer(z2, 1, (k - L2_LAG) % EXPERTS, h1_hi[r], h1_lo[r], True, True).then_inc(l2_done, 1)
                if exists(s - L3_LAG):
                    e = (k - L3_LAG) % EXPERTS
                    pe.wait_ge(h2_lo_done, s - L3_LAG + 1)
                    if e == 0:
                        wait(pe, out_done, image)
                    r = (k - L3_LAG) % 2
                    layer(y, 2, e, h2_hi[r], h2_lo[r], e == 0, e == EXPERTS - 1).then_inc(l3_done, 1)

            slots(pe, slot)

        @block.scalar
        def _(act):
            act.wait_ge(turned, 1)
            nc.scalar.mul(featT[:], y, 1.0 / IMAGES).then_inc(feat_moved, 1)
            act.wait_ge(xn2_loaded[0], 16)
            nc.scalar.copy(xs_hi[0][:], xn2[0][:]).then_inc(xs_hi_done, 1)
            act.wait_ge(step_done, 3)
            nc.scalar.activation(grown[:].rearrange("p n e -> p (n e)"), shifted[:].rearrange("p n e -> p (n e)"), ACT.Exp).then_inc(grown_done, 1)
            act.wait_ge(routeT_done, 1)
            nc.scalar.copy(routeT[:], y[0:EXPERTS, :]).then_inc(routeT_moved, 1)
            for e in range(0, EXPERTS, 2):
                act.wait_ge(spread, e + 1)
                nc.scalar.copy(route_all[:, e, :], z1[0]).then_inc(spread_moved_act, 1)
            act.wait_ge(bias_done, 1)
            nc.scalar.copy(bias_out[:], z2).then_inc(bias_moved, 1)

            def slot(s, k, image):
                if exists(s):
                    r = k % 2
                    act.wait_ge(l1_done, s + 1)
                    wait(act, l2_done, s - 1)
                    nc.scalar.activation(h1_hi[r][:], z1[r], ACT.Relu).then_inc(h1_hi_done, 1)
                if exists(s - 1):
                    r, e = (k - 1) % 2, (k - 1) % EXPERTS
                    act.wait_ge(l2_done, s)
                    wait(act, h2w_done, s - 2)
                    nc.scalar.activation(h2[r][:], z2, ACT.Relu, bias=t2[:, e:e + 1]).then_inc(h2_done, 1)
                if exists(s - 2):
                    r = k % 2
                    act.wait_ge(h2w_done, s - 1)
                    wait(act, l3_done, s - 3)
                    nc.scalar.copy(h2_hi[r][:], h2w[r][:]).then_inc(h2_hi_done, 1)
                if k % EXPERTS == 4 and exists(s + EXPERTS):
                    p = 1 - k // EXPERTS
                    act.wait_ge(xn2_loaded[p], 8 * image + (16 if p else 24))
                    wait(act, l1_done, s - 4)
                    nc.scalar.copy(xs_hi[p][:], xn2[p][:]).then_inc(xs_hi_done, 1)

            slots(act, slot)

        @block.vector
        def _(dve):
            dve.wait_ge(xs_hi_done, 1)
            nc.vector.tensor_tensor(xs_lo[0][:], xn2[0][:], xs_hi[0][:].bitcast(F32), ALU.subtract).then_inc(xs_lo_done, 1)
            dve.wait_ge(logits_done, 1)
            nc.vector.tensor_tensor(logits[:], z2[:, 0:CHUNKS * EXPERTS].rearrange("p (n e) -> p n e", e=EXPERTS),
                                    br_sb[:].unsqueeze(1).to_broadcast([128, CHUNKS, EXPERTS]), ALU.add).then_inc(step_done, 1)
            dve.wait_ge(step_done, 1)
            nc.vector.tensor_reduce(top[:], logits[:], AX.X, ALU.max).then_inc(step_done, 1)
            dve.wait_ge(step_done, 2)
            nc.vector.tensor_tensor(shifted[:], logits[:], top[:].unsqueeze(2).to_broadcast([128, CHUNKS, EXPERTS]),
                                    ALU.subtract).then_inc(step_done, 1)
            dve.wait_ge(grown_done, 1)
            nc.vector.tensor_reduce(total[:], grown[:], AX.X, ALU.add).then_inc(step_done, 1)
            dve.wait_ge(step_done, 4)
            nc.vector.reciprocal(share[:], total[:]).then_inc(step_done, 1)
            dve.wait_ge(step_done, 5)
            nc.vector.tensor_tensor(route[:], grown[:], share[:].unsqueeze(2).to_broadcast([128, CHUNKS, EXPERTS]),
                                    ALU.mult).then_inc(route_done, 1)
            for e in range(1, EXPERTS, 2):
                dve.wait_ge(spread, e + 1)
                nc.vector.tensor_copy(route_all[:, e, :], z1[1]).then_inc(spread_moved_dve, 1)
            dve.wait_ge(spread_moved_act, EXPERTS // 2)

            def slot(s, k, image):
                if exists(s):
                    r = k % 2
                    dve.wait_ge(h1_hi_done, s + 1)
                    nc.vector.scalar_tensor_tensor(out=h1_lo[r][:], in0=z1[r], scalar=0.0, in1=h1_hi[r][:].bitcast(F32),
                                                   op0=ALU.max, op1=ALU.subtract).then_inc(h1_lo_done, 1)
                if exists(s - 1):
                    r, e = (k - 1) % 2, (k - 1) % EXPERTS
                    dve.wait_ge(h2_done, s)
                    wait(dve, h2_hi_done, s - 2)
                    wait(dve, h2_lo_done, s - 2)
                    nc.vector.tensor_tensor(h2w[r][:], h2[r][:], route_all[:, e, :], ALU.mult).then_inc(h2w_done, 1)
                if exists(s - 2):
                    r = k % 2
                    dve.wait_ge(h2_hi_done, s - 1)
                    nc.vector.tensor_tensor(h2_lo[r][:], h2w[r][:], h2_hi[r][:].bitcast(F32), ALU.subtract).then_inc(h2_lo_done, 1)
                if k % EXPERTS == 2 and exists(s - EXPERTS):
                    p = 1 - k // EXPERTS
                    dve.wait_ge(l3_done, s - 2)
                    dve.wait_ge(x1_biased, image)
                    nc.vector.tensor_tensor(x1[p][:], y, x1[p][:], ALU.add).then_inc(out_done, 1)

            slots(dve, slot)

        @block.gpsimd
        def _(pool):
            pool.wait_ge(bias_moved, 1)

            def bias_x1(b, p):
                pool.wait_ge(x1_loaded[p], 8 * b + (8 if p else 16))
                nc.gpsimd.tensor_tensor(x1[p][:], x1[p][:], bias_out[:], ALU.add).then_inc(x1_biased, 1)

            def split_low(b, p):
                pool.wait_ge(xs_hi_done, b + 1)
                nc.gpsimd.tensor_tensor(xs_lo[p][:], xn2[p][:], xs_hi[p][:].bitcast(F32), ALU.subtract).then_inc(xs_lo_done, 1)

            bias_x1(0, 0)
            with pool.Fori(0, IMAGES // 2 - 1) as i:
                for p in (1, 0):
                    split_low(2 * i + (1 if p else 2), p)
                    bias_x1(2 * i + (1 if p else 2), p)
            split_low(IMAGES - 1, 1)
            bias_x1(IMAGES - 1, 1)




def kernel(x, L0_conv_w_qkv, L0_conv_w_out, L0_conv_b_out, L0_ffn_Wr, L0_ffn_br, L0_ffn_W1, L0_ffn_b1, L0_ffn_g1,
           L0_ffn_be1, L0_ffn_m1, L0_ffn_v1, L0_ffn_W2, L0_ffn_b2, L0_ffn_g2, L0_ffn_be2, L0_ffn_m2, L0_ffn_v2,
           L0_ffn_Wo, L0_ffn_bo):
    import concourse.bacc as bacc
    from concourse.bass_utils import run_bass_kernel_spmd as run

    small = np.stack([np.asarray(a) for a in (
        L0_ffn_g1, L0_ffn_v1, L0_ffn_b1, L0_ffn_m1, L0_ffn_be1,
        L0_ffn_g2, L0_ffn_v2, L0_ffn_b2, L0_ffn_m2, L0_ffn_be2)]).transpose(2, 0, 1)
    arrays = {
        "x": np.asarray(x).reshape(IMAGES, C, PIXELS),
        "w_qkv": np.asarray(L0_conv_w_qkv),
        "w_out": np.asarray(L0_conv_w_out),
        "b_out": np.asarray(L0_conv_b_out).reshape(C, 1),
        "Wr": np.asarray(L0_ffn_Wr),
        "br": np.ascontiguousarray(np.broadcast_to(np.asarray(L0_ffn_br)[None, :], (128, EXPERTS))),
        "W1": np.asarray(L0_ffn_W1),
        "W2": np.asarray(L0_ffn_W2),
        "Wo": np.asarray(L0_ffn_Wo),
        "small": np.ascontiguousarray(small),
        "bo": np.asarray(L0_ffn_bo),
        "ident": np.eye(128, dtype=np.float32),
        "heads": np.kron(np.eye(128 // HEAD_DIM), np.ones((HEAD_DIM, HEAD_DIM))).astype(np.float32),
    }
    nc = bacc.Bacc("TRN2", target_bir_lowering=False, num_devices=1)
    arrays = {f"in_{name}": np.ascontiguousarray(a) for name, a in arrays.items()}
    args = [nc.dram_tensor(name, a.shape, F32, kind="ExternalInput").ap() for name, a in arrays.items()]
    out = nc.dram_tensor("out_0", [IMAGES, C, PIXELS], F32, kind="ExternalOutput").ap()
    metaformer_kernel(nc, *args, out)
    result = run(nc, [arrays], core_ids=[0]).results[0]["out_0"]
    return result.reshape(IMAGES, C, SIDE, SIDE)
```

```python
from contextlib import ExitStack

import numpy as np

import concourse.bass as bass
from concourse import mybir

F32 = mybir.dt.float32
F32R = mybir.dt.float32r
ALU = mybir.AluOpType
ACT = mybir.ActivationFunctionType
AX = mybir.AxisListType

IMAGES, C, SIDE = 16, 128, 32
PIXELS = SIDE * SIDE
CHUNKS = PIXELS // 128
HEADS, HEAD_DIM = 8, 32
LATENT = HEADS * HEAD_DIM
EXPERTS, HIDDEN = 8, 128
BANK = 512
LN_C_EPS, LN_T_EPS, BN_EPS = 1e-6, 1e-5, 1e-3
G1, V1, B1, M1, BE1, G2, V2, B2, M2, BE2 = range(10)
S1, T1, S2 = range(3)
MINUS_HALF, BN_EPS_K, ONE_C = range(3)
CONSTANTS = {MINUS_HALF: -0.5, BN_EPS_K: BN_EPS, ONE_C: 1.0 / C}
TWO_MEAN, DIFFERENCE, SQUARES, BETWEEN, MINUS_MEAN, WITHIN, VARIANCE, RSTD, SHIFT = range(9)


def wait(engine, semaphore, count):
    if not isinstance(count, int) or count > 0:
        engine.wait_ge(semaphore, count)


def at(t, n):
    return isinstance(t, int) and t == n


def metaformer_kernel(nc, x, w_qkv, w_out, b_out, Wr, br, W1, W2, Wo, small, bo, ident_in, heads_in, out):
    SLOTS = IMAGES * EXPERTS
    L3_LAG = 3
    SPREAD = 2
    BRIDGED = 4
    x1_dram = nc.dram_tensor("x1_scratch", [IMAGES, C, PIXELS], F32, kind="Internal").ap()
    xn2_dram = nc.dram_tensor("xn2_scratch", [IMAGES, C, PIXELS], F32, kind="Internal").ap()
    route_dram = nc.dram_tensor("route_scratch", [EXPERTS, PIXELS], F32, kind="Internal").ap()

    with ExitStack() as ctx:
        def sb(name, shape, dt=F32):
            return ctx.enter_context(nc.sbuf_tensor(name, shape, dt))

        def sem(name):
            return ctx.enter_context(nc.semaphore(name))

        psum = ctx.enter_context(nc.psum_tensor("psum", [128, 8, BANK], F32))

        def banks(first, n):
            return psum[:, first:first + n, :].rearrange("p b n -> p (b n)")

        w_hi = sb("w_hi", [128, 3, EXPERTS, 128], F32R)
        w_lo = sb("w_lo", [128, 3, EXPERTS, 128], F32R)
        ident = sb("ident", [128, 128])
        t2 = sb("t2", [HIDDEN, EXPERTS])
        bo_sb = sb("bo_sb", [EXPERTS, C])
        wr_sb = sb("wr_sb", [C, EXPERTS])
        br_sb = sb("br_sb", [128, EXPERTS])
        feat = sb("feat", [128, CHUNKS, C])
        route_all = sb("route_all", [128, EXPERTS, PIXELS])

        def as_tokens(n):
            return route_all[:, n].rearrange("p (n c) -> p n c", n=CHUNKS)

        heads = sb("heads", [128, 128])
        wqkv_sb = sb("wqkv_sb", [128, 6, C])
        wout_sb = sb("wout_sb", [C, LATENT])
        bout_sb = sb("bout_sb", [C, 1])
        wkT_hi = sb("wkT_hi", [C, LATENT], F32R)
        wkT_lo = sb("wkT_lo", [C, LATENT], F32R)
        wvT = sb("wvT", [C, LATENT])
        woutT = sb("woutT", [128, 2, C])
        w_raw = sb("w_raw", [128, 3, EXPERTS, 128])
        small_sb = sb("small_sb", [HIDDEN, 10, EXPERTS])
        bn_std = sb("bn_std", [HIDDEN, 2, EXPERTS])
        bn_tmp = sb("bn_tmp", [HIDDEN, 2, EXPERTS])
        cols = sb("cols", [HIDDEN, 3, EXPERTS])
        minus_mean = sb("minus_mean", [128, 128])
        xT = sb("xT", [128, CHUNKS, C])
        x1T = sb("x1T", [128, CHUNKS, C])
        ln_wait = sb("ln_wait", [128, CHUNKS])
        const = sb("const", [128, len(CONSTANTS), CHUNKS])
        x_in = [route_all[:, p] for p in (6, 7)]
        x_res = [sb(f"x_res{p}", [C, PIXELS]) for p in range(2)]
        xnT = [as_tokens(n) for n in (4, 5)]
        xn_hi = [sb(f"xn_hi{p}", [C, PIXELS], F32R) for p in range(2)]
        xn_lo = [sb(f"xn_lo{p}", [C, PIXELS], F32R) for p in range(2)]
        ek = [route_all[:, j] for j in (0, 1)]
        ekT = [as_tokens(n) for n in (2, 3)]
        negmax = sb("negmax", [128, 2])
        rawmax = sb("rawmax", [128, 2, 2])
        sums = [sb(f"sums{p}", [128, 2]) for p in range(2)]
        rsum = sb("rsum", [128, 2])
        gT = sb("gT", [C, LATENT])
        ctxT = sb("ctxT", [128, 2, 128])
        y_sb = sb("y_sb", [128, 2, C])
        mT_hi = sb("mT_hi", [C, C], F32R)
        mT_lo = sb("mT_lo", [C, C], F32R)
        xn2T = sb("xn2T", [128, CHUNKS, C])
        xn2 = [sb(f"xn2_{p}", [C, PIXELS]) for p in range(2)]
        st = [sb(f"st{k}", [128, CHUNKS, 6]) for k in range(2)]
        ln = [sb(f"ln{k}", [128, 9, CHUNKS]) for k in range(2)]

        p_tok, p_chan, p_k, p_e, p_g = banks(0, 2), banks(2, 2), banks(4, 2), banks(6, 1), banks(7, 1)
        p_late = banks(6, 2)

        ident_loaded, small_loaded = sem("ident_loaded"), sem("small_loaded")
        attn_w = sem("attn_w")
        expert_w = sem("expert_w")
        in_loaded = [sem(f"in_loaded{p}") for p in range(2)]
        res_loaded = [sem(f"res_loaded{p}") for p in range(2)]
        x1_stored = [sem(f"x1_stored{p}") for p in range(2)]
        xn2_stored = [sem(f"xn2_stored{p}") for p in range(2)]
        const_set = sem("const_set")
        wT_done, wk_hi_done, wT_moved = sem("wT_done"), sem("wk_hi_done"), sem("wT_moved")
        bn_step, cols_done, bcast_done, scaled = sem("bn_step"), sem("cols_done"), sem("bcast_done"), sem("scaled")
        shift_done, w1_shifted, w_hi_done, w_split = sem("shift_done"), sem("w1_shifted"), sem("w_hi_done"), sem("w_split")
        k_done, ctx_done, tx_done, y_done = sem("k_done"), sem("ctx_done"), sem("tx_done"), sem("y_done")
        m_done, mx_done, e_done, g_done = sem("m_done"), sem("mx_done"), sem("e_done"), sem("g_done")
        xnt_done, x1t_done, xn2t_done = sem("xnt_done"), sem("x1t_done"), sem("xn2t_done")
        xn2_moved, exp_done, m_hi_done = sem("xn2_moved"), sem("exp_done"), sem("m_hi_done")
        e_moved, xn_hi_done = sem("e_moved"), sem("xn_hi_done")
        copy1_done, copy2_done = sem("copy1_done"), sem("copy2_done")
        g_moved, max_done, negmax_done, ctx_moved = sem("g_moved"), sem("max_done"), sem("negmax_done"), sem("ctx_moved")
        rsum_done, y_moved, stats1_done, m_lo_done = sem("rsum_done"), sem("y_moved"), sem("stats1_done"), sem("m_lo_done")
        x1_done, xn_lo_done, stats2_done, norm2_first = sem("x1_done"), sem("xn_lo_done"), sem("stats2_done"), sem("norm2_first")
        norm1_first = sem("norm1_first")
        stats_done = [stats1_done, stats2_done]
        sums_done = [sem(f"sums_done{k}") for k in range(2)]
        terms_done = [sem(f"terms_done{k}") for k in range(2)]
        var_done = [sem(f"var_done{k}") for k in range(2)]
        rstd_done = [sem(f"rstd_done{k}") for k in range(2)]
        ln_done = [sem(f"ln_done{k}") for k in range(2)]
        norm1_done, norm2_last, feat_done = sem("norm1_done"), sem("norm2_last"), sem("feat_done")

        def rounds(engine, step):
            def valid(t):
                return dict(s=t + 2 < IMAGES, a=0 <= t + 1 < IMAGES, b=0 <= t < IMAGES, c=0 <= t - 1 < IMAGES,
                            f=0 <= t - 2 < IMAGES, d=0 <= t - 3 < IMAGES)
            for t in range(-2, 5):
                step(t, t % 2, **valid(t))
            with engine.Fori(0, (IMAGES - 8) // 2) as i:
                for t in (5, 6):
                    step(2 * i + t, t % 2, s=True, a=True, b=True, c=True, f=True, d=True)
            for t in range(IMAGES - 3, IMAGES):
                step(t, t % 2, **valid(t))

        def x1_tokens(image):
            return xT if at(image, IMAGES - 1) else x1T

        def norm1_split(image):
            return 5 if at(image, 0) else 0

        def norm2_split(image):
            return 5 if isinstance(image, int) and image >= IMAGES - 3 else 3

        def last_round(step, t):
            step(t, t % 2, s=False, a=False, b=False, c=t == IMAGES, f=t <= IMAGES + 1, d=True)

        featT = xT[:].rearrange("p n c -> p (n c)")
        logits = sb("logits", [128, CHUNKS, EXPERTS])
        top = sb("top", [128, CHUNKS])
        shifted = sb("shifted", [128, CHUNKS, EXPERTS])
        grown = sb("grown", [128, CHUNKS, EXPERTS])
        total = sb("total", [128, CHUNKS])
        share = sb("share", [128, CHUNKS])
        route = sb("route", [128, CHUNKS, EXPERTS])
        routeT = sb("routeT", [EXPERTS, PIXELS])
        bias_out = x1T[:].rearrange("p n c -> p (n c)")
        xs_in = [sb(f"xs_in{p}", [C, PIXELS]) for p in range(2)]
        xs_hi = [sb(f"xs_hi{p}", [C, PIXELS], F32R) for p in range(2)]
        xs_lo = [sb(f"xs_lo{p}", [C, PIXELS], F32R) for p in range(2)]
        h1_hi = [sb(f"h1_hi{p}", [HIDDEN, PIXELS], F32R) for p in range(2)]
        h1_lo = [sb(f"h1_lo{p}", [HIDDEN, PIXELS], F32R) for p in range(2)]
        h2 = [sb(f"h2_{p}", [HIDDEN, PIXELS]) for p in range(2)]
        h2w = [w_raw[:, p].rearrange("p e h -> p (e h)") for p in range(2)]
        h2_hi = [sb(f"h2_hi{p}", [HIDDEN, PIXELS], F32R) for p in range(2)]
        h2_lo = [sb(f"h2_lo{p}", [HIDDEN, PIXELS], F32R) for p in range(2)]

        y_out = sb("y_out", [C, PIXELS])
        feat_most = y_out
        z1, z2, y = [banks(4, 2), banks(6, 2)], banks(0, 2), banks(2, 2)

        xs_loaded = [sem(f"xs_loaded{p}") for p in range(2)]
        route_stored = sem("route_stored")
        route_loaded = [sem(f"route_loaded{e}") for e in range(EXPERTS)]
        x1_loaded = [sem(f"x1_loaded{p}") for p in range(2)]
        out_stored = [sem(f"out_stored{p}") for p in range(2)]
        turned, feat_moved, logits_done, step_done = sem("turned"), sem("feat_moved"), sem("logits_done"), sem("step_done")
        grown_done, route_done, routeT_done, routeT_moved = sem("grown_done"), sem("route_done"), sem("routeT_done"), sem("routeT_moved")
        spread, spread_moved = sem("spread"), [sem(f"spread_moved{e}") for e in range(2)]
        bias_done, bias_moved, feat_most_moved = sem("bias_done"), sem("bias_moved"), sem("feat_most_moved")
        l1_done, l2_done, l3_done = sem("l1_done"), sem("l2_done"), sem("l3_done")
        h1_hi_done, h1_lo_done, h2_done = sem("h1_hi_done"), sem("h1_lo_done"), sem("h2_done")
        h2w_done, h2_hi_done, h2_lo_done = sem("h2w_done"), sem("h2_hi_done"), sem("h2_lo_done")
        y_out_moved, last_done = sem("y_out_moved"), sem("last_done")
        xs_hi_done, xs_lo_done, x1_biased, out_done = sem("xs_hi_done"), sem("xs_lo_done"), sem("x1_biased"), sem("out_done")

        def slots(engine, slot):
            period = 2 * EXPERTS
            first = L3_LAG + EXPERTS
            for s in range(BRIDGED, first):
                slot(s, s, s // EXPERTS)
            trips = (SLOTS - first) // period
            with engine.Fori(0, trips) as i:
                for k in range(first, first + period):
                    slot(period * i + k, k % period, 2 * i + k // EXPERTS)
            for s in range(first + trips * period, SLOTS + L3_LAG):
                slot(s, s % period, s // EXPERTS)

        def exists(s):
            return not isinstance(s, int) or 0 <= s < SLOTS

        block = ctx.enter_context(nc.Block())

        @block.sync
        def _(sp):
            sp.dma_start(x_in[0], x[0]).then_inc(in_loaded[0], 16)
            sp.dma_start(small_sb[:], small).then_inc(small_loaded, 16)
            sp.dma_start(ident[:], ident_in).then_inc(ident_loaded, 16)
            sp.dma_start(wqkv_sb[:], w_qkv.rearrange("(t p) c -> p t c", p=128)).then_inc(attn_w, 16)
            sp.dma_start(wout_sb[:], w_out).then_inc(attn_w, 16)
            sp.dma_start(heads[:], heads_in).then_inc(attn_w, 16)
            sp.dma_start(bout_sb[:], b_out).then_inc(attn_w, 16)
            sp.dma_start(x_in[1], x[1]).then_inc(in_loaded[1], 16)
            sp.dma_start(bo_sb[:], bo).then_inc(expert_w, 16)
            sp.dma_start(wr_sb[:], Wr).then_inc(expert_w, 16)
            sp.dma_start(br_sb[:], br).then_inc(expert_w, 16)
            for k, w in enumerate((W1, W2, Wo)):
                sp.dma_start(w_raw[:, k], w.rearrange("e c h -> c e h")).then_inc(expert_w, 16)

            def step(t, p, s, a, b, c, f, d):
                q = 1 - p
                if not isinstance(t, int) or -1 <= t < IMAGES - 3:
                    sp.wait_ge(tx_done, t + 2)
                    sp.dma_start(x_in[q], x[t + 3]).then_inc(in_loaded[q], 16)
                if at(t, IMAGES - 2):
                    for r in range(2):
                        sp.wait_ge(xn2_stored[r], 16)
                        sp.dma_start(xs_in[r][:], xn2_dram[r]).then_inc(xs_loaded[r], 16)
                if b:
                    if not isinstance(t, int) or t >= 2:
                        sp.wait_ge(x1t_done, t - 1)
                        sp.wait_ge(x1_stored[p], 8 * t - 8 * p)
                    sp.dma_start(x_res[p][:], x[t]).then_inc(res_loaded[p], 16)
                if d:
                    sp.wait_ge(xn2_moved, t - 2)
                    sp.dma_start(xn2_dram[t - 3], xn2[q][:]).then_inc(xn2_stored[q], 16)
                if c:
                    sp.wait_ge(x1_done, t)
                    sp.dma_start(x1_dram[t - 1], x_res[q][:]).then_inc(x1_stored[q], 16)

            rounds(sp, step)
            for t in range(IMAGES, IMAGES + 3):
                last_round(step, t)
            sp.wait_ge(routeT_moved, 1)
            sp.dma_start(route_dram, routeT[:]).then_inc(route_stored, 16)
            sp.wait_ge(route_stored, 16)
            for e in range(SPREAD, EXPERTS):
                sp.dma_start(route_all[:, e, :], route_dram[e:e + 1, :].to_broadcast([128, PIXELS])).then_inc(route_loaded[e], 16)
            for p in range(2):
                sp.wait_ge(x1_stored[p], 16 * (IMAGES // 2))
                sp.wait_ge(xn2_stored[p], 16 * (IMAGES // 2))
                sp.wait_ge(x1t_done, IMAGES)
                sp.dma_start(x_res[p][:], x1_dram[p]).then_inc(x1_loaded[p], 16)

            def load(b, p):
                sp.wait_ge(xs_lo_done, b - 1)
                sp.wait_ge(xs_hi_done, b - 1)
                sp.dma_start(xs_in[p][:], xn2_dram[b]).then_inc(xs_loaded[p], 16)
                sp.wait_ge(out_done, b - 1)
                sp.dma_start(out[b - 2], x_res[p][:]).then_inc(out_stored[p], 16)
                sp.wait_ge(out_stored[p], 8 * b - 8 * p)
                sp.dma_start(x_res[p][:], x1_dram[b]).then_inc(x1_loaded[p], 16)

            with sp.Fori(0, IMAGES // 2 - 1) as i:
                for p in range(2):
                    load(2 * i + (2 + p), p)
            sp.wait_ge(out_done, IMAGES - 1)
            sp.dma_start(out[IMAGES - 2], x_res[0][:]).then_inc(out_stored[0], 16)
            sp.wait_ge(out_stored[0], 16 * (IMAGES // 2))
            for n in range(2):
                sp.wait_ge(last_done, n + 1)
                px = slice(BANK * n, BANK * (n + 1))
                sp.dma_start(out[IMAGES - 1][:, px], x_res[1][:, px]).then_inc(out_stored[n], 16)
            sp.wait_ge(out_stored[0], 16 * (IMAGES // 2 + 1))
            sp.wait_ge(out_stored[1], 16 * (IMAGES // 2))

        @block.tensor
        def _(pe):
            pe.wait_ge(ident_loaded, 16)

            def step(t, p, s, a, b, c, f, d):
                q = 1 - p
                if b:
                    k_half(t, p, 0)
                if at(t, 0):
                    shift_weights()
                if c:
                    pe.wait_ge(g_moved, t)
                    for j in range(2):
                        half = slice(128 * j, 128 * (j + 1))
                        mm = pe.matmul(p_g[:, 256 + 128 * j:256 + 128 * (j + 1)], wvT[:, half], gT[:, half], start=True, stop=True)
                    mm.then_inc(ctx_done, 1)
                if f:
                    pe.wait_ge(x1_done, t - 1)
                    if not isinstance(t, int) or t + 1 < IMAGES:
                        pe.wait_ge(copy1_done, t + 2)
                    else:
                        pe.wait_ge(copy2_done, t - 2)
                    turn(p_tok, lambda n: x_res[p][:, 128 * n:128 * (n + 1)]).then_inc(x1t_done, 1)
                if d:
                    pe.wait_ge(norm2_first, t - 2)
                    pe.wait_ge(norm2_last, t - 2)
                    wait(pe, xn2_moved, t - 3)
                    turn(p_chan, lambda n: xn2T[:, n, :]).then_inc(xn2t_done, 1)
                if c:
                    pe.wait_ge(ctx_moved, t)
                    for j in range(2):
                        mm = pe.matmul(p_g[:, 128 * j:128 * (j + 1)], ctxT[:, j, :], woutT[:, j, :], start=True, stop=True)
                    mm.then_inc(y_done, 1)
                if b:
                    k_half(t, p, 1)
                if at(t, IMAGES):
                    pe.wait_ge(exp_done, 2 * IMAGES)
                    layer1(0, 0, 0)
                if c:
                    pe.wait_ge(y_moved, t)
                    for j in range(2):
                        mm = pe.matmul(p_g[:, 256:384], wqkv_sb[:, j, :], y_sb[:, j, :], start=j == 0, stop=j == 1)
                    mm.then_inc(m_done, 1)
                if b:
                    turn_e(t, 0, 0)
                if s:
                    pe.wait_ge(in_loaded[p], 8 * t + (24 if p else 32))
                    if f:
                        pe.wait_ge(copy2_done, t - 1)
                    else:
                        wait(pe, copy1_done, t + 2)
                    turn(p_tok, lambda n: x_in[p][:, 128 * n:128 * (n + 1)]).then_inc(tx_done, 1)
                if at(t, -2):
                    pe.wait_ge(attn_w, 4 * 16)
                    for k in range(4):
                        pe.transpose(p_chan[:, 128 * k:128 * (k + 1)], wqkv_sb[:, 2 + k, :], ident[:])
                    for j in range(2):
                        mm = pe.transpose(p_chan[:, BANK + 128 * j:BANK + 128 * (j + 1)],
                                          wout_sb[:, 128 * j:128 * (j + 1)], ident[:])
                    mm.then_inc(wT_done, 1)
                if c:
                    pe.wait_ge(m_lo_done, t)
                    wait(pe, xn2_moved, t - 2)
                    for n in range(2):
                        px = slice(BANK * n, BANK * (n + 1))
                        pe.matmul(p_chan[:, px], mT_hi[:], xn_hi[q][:, px], start=True, stop=False)
                        pe.matmul(p_chan[:, px], mT_hi[:], xn_lo[q][:, px], start=False, stop=False)
                        mm = pe.matmul(p_chan[:, px], mT_lo[:], xn_hi[q][:, px], start=False, stop=True)
                    mm.then_inc(mx_done, 1)
                if b:
                    turn_e(t, 0, 1)
                    add_g(t, p, 0, 0)
                    turn_e(t, 1, 0)
                if at(t, -1):
                    pe.wait_ge(cols_done, 1)
                    spread_scales(p_k, S1)
                    spread_scales(p_late, S2)
                if a:
                    pe.wait_ge(norm1_done, t + 2)
                    if at(t, -1):
                        pe.wait_ge(norm1_first, 1)
                        pe.wait_ge(wT_moved, 1)
                    wait(pe, x1_done, t)
                    turn(p_chan, lambda n: xnT[q][:, n, :]).then_inc(xnt_done, 1)
                if b:
                    add_g(t, p, 0, 1)
                    turn_e(t, 1, 1)
                    add_g(t, p, 1, 0)
                    add_g(t, p, 1, 1)

            def spread_scales(dst, col):
                for e in range(EXPERTS):
                    mm = pe.transpose(dst[:, 128 * e:128 * (e + 1)], cols[:, col, e:e + 1].to_broadcast([128, 128]), ident[:])
                mm.then_inc(bcast_done, 1)

            def shift_weights():
                pe.wait_ge(scaled, 2)
                for e in range(EXPERTS):
                    pe.matmul(p_late[:, 128 * e:128 * (e + 1)], minus_mean[:], w_raw[:, 0, e, :], start=True, stop=False)
                    mm = pe.matmul(p_late[:, 128 * e:128 * (e + 1)], cols[:, T1, e:e + 1].to_broadcast([128, 128]), ident[:],
                                   start=False, stop=True)
                mm.then_inc(shift_done, 1)

            def turn(dst, chunk):
                return turn_part(dst, 128, chunk)

            def turn_part(dst, rows, chunk):
                for n in range(CHUNKS):
                    mm = pe.transpose(dst[0:rows, 128 * n:128 * (n + 1)], chunk(n), ident[:])
                return mm

            def k_half(t, p, j):
                half = slice(128 * j, 128 * (j + 1))
                if j == 0:
                    pe.wait_ge(xn_lo_done, t + 1)
                wait(pe, exp_done, 2 * t + j)
                for n in range(2):
                    px = slice(BANK * n, BANK * (n + 1))
                    for w, xs in ((wkT_hi, xn_hi), (wkT_lo, xn_hi), (wkT_hi, xn_lo)):
                        mm = pe.matmul(p_k[:, px], w[:, half], xs[p][:, px],
                                       start=w is wkT_hi and xs is xn_hi, stop=xs is xn_lo)
                    mm.then_inc(k_done, 1)

            def turn_e(t, j, h):
                if h == 0:
                    pe.wait_ge(exp_done, 2 * t + j + 1)
                if isinstance(t, int) and t == j == h == 0:
                    pe.wait_ge(w1_shifted, 1)
                wait(pe, e_moved, 4 * t + 2 * j + h)
                for n in range(4):
                    chunk = 4 * h + n
                    mm = pe.transpose(p_e[:, 128 * n:128 * (n + 1)], ek[j][:, 128 * chunk:128 * (chunk + 1)], ident[:])
                mm.then_inc(e_done, 1)

            def add_g(t, p, j, h):
                pe.wait_ge(e_moved, 4 * t + 2 * j + h + 1)
                for n in range(4):
                    chunk = 4 * h + n
                    mm = pe.matmul(p_g[:, 128 * j:128 * (j + 1)], xnT[p][:, chunk, :], ekT[j][:, chunk, :],
                                   start=chunk == 0, stop=chunk == CHUNKS - 1)
                if (j, h) == (1, 1):
                    mm.then_inc(g_done, 1)

            def layer(dst, which, e, hi, lo, first, last):
                for w, part in ((w_hi, hi), (w_lo, hi), (w_hi, lo)):
                    for n in range(2):
                        px = slice(BANK * n, BANK * (n + 1))
                        mm = pe.matmul(dst[:, px], w[:, which, e, :], part[:, px],
                                       start=first and w is w_hi and part is hi, stop=last and part is lo, skip_group_check=True)
                return mm

            def layer1(s, k, image):
                e, p = k % EXPERTS, k // EXPERTS
                if e == 0:
                    pe.wait_ge(xs_lo_done, image + 1)
                wait(pe, h1_lo_done, s - 1)
                layer(z1[k % 2], 0, e, xs_hi[p], xs_lo[p], True, True).then_inc(l1_done, 1)

            def layer2(s, k):
                pe.wait_ge(h1_lo_done, s + 1)
                wait(pe, h2_done, s)
                layer(z2, 1, k % EXPERTS, h1_hi[k % 2], h1_lo[k % 2], True, True).then_inc(l2_done, 1)

            def layer3(s, k, image):
                e, r = (k - L3_LAG) % EXPERTS, (k - L3_LAG) % 2
                pe.wait_ge(h2_lo_done, s - L3_LAG + 1)
                if e == 0:
                    wait(pe, y_out_moved, image)
                if isinstance(s, int) and s == SLOTS - 1 + L3_LAG:
                    for n in range(2):
                        px = slice(BANK * n, BANK * (n + 1))
                        for w, part in ((w_hi, h2_hi), (w_lo, h2_hi), (w_hi, h2_lo)):
                            mm = pe.matmul(y[:, px], w[:, 2, e, :], part[r][:, px], start=False, stop=part is h2_lo,
                                           skip_group_check=True)
                        mm.then_inc(l3_done, 1)
                else:
                    layer(y, 2, e, h2_hi[r], h2_lo[r], e == 0, e == EXPERTS - 1).then_inc(l3_done, 1)

            rounds(pe, step)
            last_round(step, IMAGES)
            layer1(1, 1, 0)
            last_round(step, IMAGES + 1)
            pe.wait_ge(copy2_done, IMAGES)
            layer2(0, 0)
            layer1(2, 2, 0)
            pe.wait_ge(feat_done, IMAGES - 1)
            pe.wait_ge(xn2_moved, IMAGES - 1)
            turn(p_chan, lambda n: feat[:, n, :]).then_inc(turned, 1)
            pe.wait_ge(feat_most_moved, 1)
            last_round(step, IMAGES + 2)
            layer2(1, 1)
            pe.wait_ge(h1_lo_done, 3)
            pe.wait_ge(feat_moved, 1)
            for n in range(CHUNKS):
                mm = pe.matmul(z1[0][:, EXPERTS * n:EXPERTS * (n + 1)], featT[:, 128 * n:128 * (n + 1)], wr_sb[:], start=True, stop=True)
            mm.then_inc(logits_done, 1)
            layer1(3, 3, 0)
            pe.wait_ge(xn2_moved, IMAGES)
            pe.wait_ge(route_done, 1)
            turn_part(y, EXPERTS, lambda n: route[:, n, :]).then_inc(routeT_done, 1)
            turn(z1[0], lambda n: route[:, n, 0:1].to_broadcast([128, 128])).then_inc(spread, 1)
            pe.wait_ge(routeT_moved, 1)
            turn(y, lambda n: route[:, n, 1:2].to_broadcast([128, 128])).then_inc(spread, 1)
            pe.wait_ge(h2_done, 2)
            for n in range(2):
                mm = pe.matmul(z2[:, BANK * n:BANK * (n + 1)], bo_sb[:], routeT[:, BANK * n:BANK * (n + 1)], start=True, stop=True)
            mm.then_inc(bias_done, 1)
            pe.wait_ge(spread_moved[1], 1)
            layer3(3, 3, 0)
            pe.wait_ge(bias_moved, 1)
            layer2(2, 2)
            pe.wait_ge(spread_moved[0], 1)

            def slot(s, k, image):
                if exists(s):
                    layer1(s, k, image)
                if exists(s - 1):
                    layer2(s - 1, k - 1)
                if exists(s - L3_LAG):
                    layer3(s, k, image)

            slots(pe, slot)

        @block.scalar
        def _(act):
            def expert_weights_high(k):
                nc.scalar.copy(w_hi[:, k].rearrange("p e h -> p (e h)"),
                               w_raw[:, k].rearrange("p e h -> p (e h)")).then_inc(w_hi_done, 1)

            def step(t, p, s, a, b, c, f, d):
                q = 1 - p
                if at(t, -1):
                    act.wait_ge(expert_w, 6 * 16)
                    expert_weights_high(2)
                if at(t, 0):
                    act.wait_ge(scaled, 2)
                    expert_weights_high(1)
                if c:
                    act.wait_ge(g_done, t)
                    wait(act, ctx_done, t - 1)
                    nc.scalar.copy(gT[:], p_g[:, 0:LATENT]).then_inc(g_moved, 1)
                if b:
                    exp_half(t, p, 0)
                if at(t, 0):
                    act.wait_ge(w1_shifted, 1)
                    expert_weights_high(0)
                if f:
                    act.wait_ge(x1t_done, t - 1)
                    if x1_tokens(t - 2) is x1T:
                        wait(act, norm2_first, t - 2)
                        wait(act, norm2_last, t - 2)
                    else:
                        act.wait_ge(norm1_done, IMAGES)
                    nc.scalar.copy(x1_tokens(t - 2)[:], p_tok).then_inc(copy2_done, 1)
                if d:
                    act.wait_ge(xn2t_done, t - 2)
                    if not isinstance(t, int) or t >= 5:
                        act.wait_ge(xn2_stored[q], 8 * t - 24 - 8 * q)
                    nc.scalar.activation(xn2[q][:], p_chan, ACT.Copy, bias=1.0).then_inc(xn2_moved, 1)
                if c:
                    act.wait_ge(m_done, t)
                    wait(act, mx_done, t - 1)
                    nc.scalar.copy(mT_hi[:], p_g[:, 256:384]).then_inc(m_hi_done, 1)
                if b:
                    move_e(t, 0, 0)
                    exp_half(t, p, 1)
                if s:
                    act.wait_ge(tx_done, t + 3)
                    wait(act, norm1_done, t + 2)
                    if at(t, -1):
                        act.wait_ge(norm1_first, 1)
                    nc.scalar.copy(xT[:], p_tok).then_inc(copy1_done, 1)
                if at(t, -2):
                    act.wait_ge(wT_done, 1)
                    nc.scalar.copy(wkT_hi[:], p_chan[:, 0:LATENT]).then_inc(wk_hi_done, 1)
                if at(t, IMAGES - 1):
                    act.wait_ge(xs_loaded[0], 16)
                    nc.scalar.copy(xs_hi[0][:], xs_in[0][:]).then_inc(xs_hi_done, 1)
                if b:
                    move_e(t, 0, 1)
                    move_e(t, 1, 0)
                if a:
                    act.wait_ge(xnt_done, t + 2)
                    wait(act, mx_done, t)
                    nc.scalar.copy(xn_hi[q][:], p_chan).then_inc(xn_hi_done, 1)
                if b:
                    move_e(t, 1, 1)

            def move_e(t, j, h):
                act.wait_ge(e_done, 4 * t + 2 * j + h + 1)
                wait(act, g_done, t)
                nc.scalar.copy(ekT[j][:, 4 * h:4 * h + 4, :].rearrange("p n d -> p (n d)"), p_e).then_inc(e_moved, 1)

            def exp_half(t, p, j):
                act.wait_ge(negmax_done, 2 * t + j + 1)
                wait(act, e_done, 4 * t + 2 * j - 2)
                if j == 0:
                    wait(act, rsum_done, t - 1)
                nc.scalar.activation(ek[j], p_k, ACT.Exp, bias=negmax[:, j:j + 1],
                                     accum_out=sums[p][:, j:j + 1]).then_inc(exp_done, 1)

            def h1_high(s, k):
                r = k % 2
                act.wait_ge(l1_done, s + 1)
                wait(act, l2_done, s - 1)
                nc.scalar.activation(h1_hi[r][:], z1[r], ACT.Relu).then_inc(h1_hi_done, 1)

            def hidden2(s, k):
                r, e = k % 2, k % EXPERTS
                act.wait_ge(l2_done, s + 1)
                wait(act, h2w_done, s - 1)
                nc.scalar.activation(h2[r][:], z2, ACT.Relu, bias=t2[:, e:e + 1]).then_inc(h2_done, 1)

            def h2_high(s, k):
                r = k % 2
                act.wait_ge(h2w_done, s + 1)
                wait(act, l3_done, s - 1)
                nc.scalar.copy(h2_hi[r][:], h2w[r]).then_inc(h2_hi_done, 1)

            rounds(act, step)
            last_round(step, IMAGES)
            h1_high(0, 0)
            last_round(step, IMAGES + 1)
            h1_high(1, 1)
            hidden2(0, 0)
            act.wait_ge(turned, 1)
            nc.scalar.mul(feat_most[:], p_chan, 1.0 / IMAGES).then_inc(feat_most_moved, 1)
            h1_high(2, 2)
            act.wait_ge(feat_moved, 1)
            last_round(step, IMAGES + 2)
            hidden2(1, 1)
            act.wait_ge(step_done, 3)
            nc.scalar.activation(grown[:].rearrange("p n e -> p (n e)"), shifted[:].rearrange("p n e -> p (n e)"), ACT.Exp).then_inc(grown_done, 1)
            act.wait_ge(routeT_done, 1)
            nc.scalar.copy(routeT[:], y[0:EXPERTS, :]).then_inc(routeT_moved, 1)
            h2_high(0, 0)
            act.wait_ge(spread, 2)
            nc.scalar.copy(route_all[:, 1, :], y).then_inc(spread_moved[1], 1)
            act.wait_ge(bias_done, 1)
            nc.scalar.copy(bias_out, z2).then_inc(bias_moved, 1)
            nc.scalar.copy(route_all[:, 0, :], z1[0]).then_inc(spread_moved[0], 1)
            h1_high(3, 3)
            hidden2(2, 2)
            h2_high(1, 1)

            def slot(s, k, image):
                if k % EXPERTS == 3 and exists(s - EXPERTS):
                    act.wait_ge(l3_done, s - 3)
                    wait(act, out_done, image - 1)
                    nc.scalar.copy(y_out[:], y).then_inc(y_out_moved, 1)
                if exists(s):
                    h1_high(s, k)
                if exists(s - 1):
                    hidden2(s - 1, k - 1)
                if exists(s - 2):
                    h2_high(s - 2, k - 2)
                if k % EXPERTS == 4 and exists(s + EXPERTS):
                    p = 1 - k // EXPERTS
                    act.wait_ge(xs_loaded[p], 8 * image + (16 if p else 24))
                    wait(act, l1_done, s - 4)
                    nc.scalar.copy(xs_hi[p][:], xs_in[p][:]).then_inc(xs_hi_done, 1)

            slots(act, slot)

        @block.vector
        def _(dve):
            flat = [w_raw[:, k].rearrange("p e h -> p (e h)") for k in range(3)]

            def low_part(k, count):
                dve.wait_ge(w_hi_done, count)
                nc.vector.tensor_tensor(w_lo[:, k].rearrange("p e h -> p (e h)"), flat[k],
                                        w_hi[:, k].rearrange("p e h -> p (e h)").bitcast(F32), ALU.subtract).then_inc(w_split, 1)

            def step(t, p, s, a, b, c, f, d):
                q = 1 - p
                if at(t, -1):
                    dve.wait_ge(ln_done[0], 1)
                    for n in range(norm1_split(0)):
                        ins = nc.vector.tensor_scalar(xnT[0][:, n, :], xT[:, n, :], ln[0][:, RSTD, n:n + 1],
                                                      ln[0][:, SHIFT, n:n + 1], ALU.mult, ALU.add)
                    ins.then_inc(norm1_first, 1)
                    dve.wait_ge(expert_w, 6 * 16)
                    for k, scales in enumerate((p_k, p_late)):
                        dve.wait_ge(bcast_done, k + 1)
                        nc.vector.tensor_tensor(flat[k], flat[k], scales, ALU.mult).then_inc(scaled, 1)
                if d:
                    dve.wait_ge(ln_done[1], t - 2)
                    wait(dve, xn2t_done, t - 3)
                    wait(dve, feat_done, t - 3)
                    for n in range(norm2_split(t - 3)):
                        ins = nc.vector.tensor_scalar(xn2T[:, n, :], x1_tokens(t - 3)[:, n, :], ln[1][:, RSTD, n:n + 1],
                                                      ln[1][:, SHIFT, n:n + 1], ALU.mult, ALU.add)
                    ins.then_inc(norm2_first, 1)
                if at(t, IMAGES + 1):
                    h1_low(0, 0)
                if b:
                    head_max(t, 0)
                if at(t, 0):
                    low_part(2, 1)
                    low_part(1, 2)
                    dve.wait_ge(shift_done, 1)
                    dve.wait_ge(scaled, 1)
                    nc.vector.tensor_tensor(flat[0], flat[0], p_late, ALU.add).then_inc(w1_shifted, 1)
                if c:
                    dve.wait_ge(ctx_done, t)
                    wait(dve, y_done, t - 1)
                    for j in range(2):
                        ins = nc.vector.tensor_tensor(ctxT[:, j, :], p_g[:, 256 + 128 * j:256 + 128 * (j + 1)], heads[:], ALU.mult)
                    ins.then_inc(ctx_moved, 1)
                    dve.wait_ge(exp_done, 2 * t)
                    nc.vector.reciprocal(rsum[:], sums[q][:]).then_inc(rsum_done, 1)
                    dve.wait_ge(rsum_done, t)
                    dve.wait_ge(y_done, t)
                    wait(dve, m_done, t - 1)
                    for j in range(2):
                        ins = nc.vector.tensor_scalar(y_sb[:, j, :], p_g[:, 128 * j:128 * (j + 1)], rsum[:, j:j + 1], None, ALU.mult)
                    ins.then_inc(y_moved, 1)
                if b:
                    head_max(t, 1)
                if f and not b:
                    halves(1, x1_tokens(t - 2), t - 2)
                if c:
                    dve.wait_ge(m_hi_done, t)
                    nc.vector.tensor_tensor(mT_lo[:], p_g[:, 256:384], mT_hi[:].bitcast(F32), ALU.subtract).then_inc(m_lo_done, 1)
                if f and b:
                    halves(1, x1_tokens(t - 2), t - 2)
                if f and not b:
                    statistics(1, t - 2, LN_T_EPS)
                if c:
                    dve.wait_ge(mx_done, t)
                    dve.wait_ge(res_loaded[q], 8 * t + (0 if q else 8))
                    nc.vector.scalar_tensor_tensor(out=x_res[q][:], in0=p_chan, scalar=bout_sb[:, 0:1], in1=x_res[q][:],
                                                   op0=ALU.add, op1=ALU.add).then_inc(x1_done, 1)
                if f and b:
                    statistics(1, t - 2, LN_T_EPS)
                if s and b:
                    halves(0, xT, t + 2)
                if a:
                    dve.wait_ge(xn_hi_done, t + 2)
                    nc.vector.tensor_tensor(xn_lo[q][:], p_chan, xn_hi[q][:].bitcast(F32), ALU.subtract).then_inc(xn_lo_done, 1)
                if s and not b:
                    halves(0, xT, t + 2)
                if s:
                    statistics(0, t + 2, LN_C_EPS)
                if at(t, 0):
                    low_part(0, 3)
                if at(t, -2):
                    dve.wait_ge(wk_hi_done, 1)
                    nc.vector.tensor_tensor(wkT_lo[:], p_chan[:, 0:LATENT], wkT_hi[:].bitcast(F32), ALU.subtract)
                    nc.vector.tensor_copy(wvT[:], p_chan[:, LATENT:2 * LATENT])
                    nc.vector.tensor_copy(woutT[:].rearrange("p j c -> p (j c)"), p_chan[:, BANK:BANK + LATENT]).then_inc(wT_moved, 1)

            def halves(k, tokens, image):
                dve.wait_ge((copy1_done, copy2_done)[k], image + 1)
                for n in range(CHUNKS):
                    ins = nc.vector.bn_stats(st[k][:, n, :], tokens[:, n, :])
                ins.then_inc(stats_done[k], 1)

            def statistics(k, image, eps):
                h, o = st[k], ln[k]
                dve.wait_ge(stats_done[k], image + 1)
                wait(dve, ln_done[k], image)
                nc.vector.tensor_tensor(o[:, TWO_MEAN], h[:, :, 1], h[:, :, 4], ALU.add)
                nc.vector.tensor_tensor(o[:, DIFFERENCE], h[:, :, 1], h[:, :, 4], ALU.subtract)
                nc.vector.tensor_tensor(o[:, SQUARES], h[:, :, 2], h[:, :, 5], ALU.add).then_inc(sums_done[k], 1)
                dve.wait_ge(sums_done[k], image + 1)
                nc.vector.scalar_tensor_tensor(out=o[:, BETWEEN], in0=o[:, DIFFERENCE], scalar=0.25, in1=o[:, DIFFERENCE],
                                               op0=ALU.mult, op1=ALU.mult)
                nc.vector.tensor_scalar(o[:, MINUS_MEAN], o[:, TWO_MEAN], -0.5, None, ALU.mult)
                nc.vector.tensor_scalar(o[:, WITHIN], o[:, SQUARES], 1.0 / C, eps, ALU.mult, ALU.add).then_inc(terms_done[k], 1)
                dve.wait_ge(terms_done[k], image + 1)
                nc.vector.tensor_tensor(o[:, VARIANCE], o[:, WITHIN], o[:, BETWEEN], ALU.add).then_inc(var_done[k], 1)

            def head_max(t, j):
                for n in range(2):
                    dve.wait_ge(k_done, 4 * t + 2 * j + n + 1)
                    nc.vector.tensor_reduce(rawmax[:, j, n:n + 1], p_k[:, BANK * n:BANK * (n + 1)], AX.X, ALU.max).then_inc(max_done, 1)
                dve.wait_ge(max_done, 4 * t + 2 * j + 2)
                wait(dve, exp_done, 2 * t + j - 1)
                nc.vector.tensor_scalar(negmax[:, j:j + 1], rawmax[:, j, 0:1], rawmax[:, j, 1:2], -1.0,
                                        ALU.max, ALU.mult).then_inc(negmax_done, 1)

            def h1_low(s, k):
                r = k % 2
                dve.wait_ge(h1_hi_done, s + 1)
                nc.vector.scalar_tensor_tensor(out=h1_lo[r][:], in0=z1[r], scalar=0.0, in1=h1_hi[r][:].bitcast(F32),
                                               op0=ALU.max, op1=ALU.subtract).then_inc(h1_lo_done, 1)

            def weigh(s, k):
                r, e = k % 2, k % EXPERTS
                dve.wait_ge(h2_done, s + 1)
                if isinstance(s, int) and s < EXPERTS:
                    dve.wait_ge(*((spread_moved[1], 1) if s == 1 else (route_loaded[s], 16)))
                wait(dve, h2_hi_done, s - 1)
                wait(dve, h2_lo_done, s - 1)
                nc.vector.tensor_tensor(h2w[r], h2[r][:], route_all[:, e, :], ALU.mult).then_inc(h2w_done, 1)

            def h2_low(s, k):
                r = k % 2
                dve.wait_ge(h2_hi_done, s + 1)
                nc.vector.tensor_tensor(h2_lo[r][:], h2w[r], h2_hi[r][:].bitcast(F32), ALU.subtract).then_inc(h2_lo_done, 1)

            rounds(dve, step)
            last_round(step, IMAGES)
            last_round(step, IMAGES + 1)
            h1_low(1, 1)
            last_round(step, IMAGES + 2)
            h1_low(2, 2)
            dve.wait_ge(xn2t_done, IMAGES)
            dve.wait_ge(feat_most_moved, 1)
            nc.vector.scalar_tensor_tensor(out=featT, in0=p_chan, scalar=1.0 / IMAGES, in1=feat_most[:],
                                           op0=ALU.mult, op1=ALU.add).then_inc(feat_moved, 1)
            dve.wait_ge(logits_done, 1)
            nc.vector.tensor_tensor(logits[:], z1[0][:, 0:CHUNKS * EXPERTS].rearrange("p (n e) -> p n e", e=EXPERTS),
                                    br_sb[:].unsqueeze(1).to_broadcast([128, CHUNKS, EXPERTS]), ALU.add).then_inc(step_done, 1)
            dve.wait_ge(step_done, 1)
            nc.vector.tensor_reduce(top[:], logits[:], AX.X, ALU.max).then_inc(step_done, 1)
            dve.wait_ge(step_done, 2)
            nc.vector.tensor_tensor(shifted[:], logits[:], top[:].unsqueeze(2).to_broadcast([128, CHUNKS, EXPERTS]),
                                    ALU.subtract).then_inc(step_done, 1)
            dve.wait_ge(grown_done, 1)
            nc.vector.tensor_reduce(total[:], grown[:], AX.X, ALU.add).then_inc(step_done, 1)
            dve.wait_ge(step_done, 4)
            nc.vector.reciprocal(share[:], total[:]).then_inc(step_done, 1)
            dve.wait_ge(step_done, 5)
            nc.vector.tensor_tensor(route[:], grown[:], share[:].unsqueeze(2).to_broadcast([128, CHUNKS, EXPERTS]),
                                    ALU.mult).then_inc(route_done, 1)
            dve.wait_ge(h2_done, 1)
            dve.wait_ge(spread, 1)
            nc.vector.tensor_tensor(h2w[0], h2[0][:], z1[0], ALU.mult).then_inc(h2w_done, 1)
            h2_low(0, 0)
            weigh(1, 1)
            h1_low(3, 3)
            weigh(2, 2)
            h2_low(1, 1)

            def slot(s, k, image):
                if exists(s):
                    h1_low(s, k)
                if exists(s - 1):
                    weigh(s - 1, k - 1)
                if exists(s - 2):
                    h2_low(s - 2, k - 2)

            slots(dve, slot)
            dve.wait_ge(x1_biased, IMAGES)
            for n in range(2):
                dve.wait_ge(l3_done, SLOTS + n)
                px = slice(BANK * n, BANK * (n + 1))
                nc.vector.tensor_tensor(x_res[1][:, px], y[:, px], x_res[1][:, px], ALU.add).then_inc(last_done, 1)

        @block.gpsimd
        def _(pool):
            nc.gpsimd.memset(minus_mean[:], -1.0 / 128).then_inc(const_set, 1)
            nc.gpsimd.memset(feat[:], 0.0).then_inc(const_set, 1)
            for k, value in CONSTANTS.items():
                nc.gpsimd.memset(const[:, k], value).then_inc(const_set, 1)
            pool.wait_ge(const_set, 2 + len(CONSTANTS))

            steps = [0]

            def bn(ins):
                steps[0] += 1
                ins.then_inc(bn_step, 1)
                pool.wait_ge(bn_step, steps[0])

            pool.wait_ge(small_loaded, 16)
            for k, (g, v, b, m, be, s) in enumerate(((G1, V1, B1, M1, BE1, S1), (G2, V2, B2, M2, BE2, S2))):
                bn(nc.gpsimd.tensor_tensor(bn_std[:, k], small_sb[:, v], const[:, BN_EPS_K], ALU.add))
                bn(nc.gpsimd.tensor_tensor(bn_tmp[:, k], bn_std[:, k], const[:, MINUS_HALF], ALU.pow))
                bn(nc.gpsimd.tensor_tensor(cols[:, s], bn_tmp[:, k], small_sb[:, g], ALU.mult))
                bn(nc.gpsimd.tensor_tensor(bn_std[:, k], small_sb[:, b], small_sb[:, m], ALU.subtract))
                bn(nc.gpsimd.tensor_tensor(bn_tmp[:, k], bn_std[:, k], cols[:, s], ALU.mult))
                if k == 0:
                    bn(nc.gpsimd.tensor_tensor(bn_std[:, k], bn_tmp[:, k], small_sb[:, be], ALU.add))
                    bn(nc.gpsimd.tensor_tensor(cols[:, T1], bn_std[:, k], const[:, ONE_C], ALU.mult))
                else:
                    nc.gpsimd.tensor_tensor(t2[:], bn_tmp[:, k], small_sb[:, be], ALU.add).then_inc(cols_done, 1)

            def statistics(k, image):
                o = ln[k]
                pool.wait_ge(var_done[k], image + 1)
                nc.gpsimd.tensor_tensor(o[:, RSTD], o[:, VARIANCE], const[:, MINUS_HALF], ALU.pow).then_inc(rstd_done[k], 1)
                pool.wait_ge(rstd_done[k], image + 1)
                nc.gpsimd.tensor_tensor(o[:, SHIFT], o[:, MINUS_MEAN], o[:, RSTD], ALU.mult).then_inc(ln_done[k], 1)

            def norm(k, dst, src, chunks, done):
                nc.gpsimd.tensor_tensor(ln_wait[:], const[:, ONE_C], const[:, ONE_C], ALU.add)
                for n in chunks:
                    ins = nc.gpsimd.tensor_scalar(dst[:, n, :], src[:, n, :], ln[k][:, RSTD, n:n + 1], ln[k][:, SHIFT, n:n + 1],
                                                  ALU.mult, ALU.add)
                ins.then_inc(done, 1)

            def split_low(b, p):
                pool.wait_ge(xs_hi_done, b + 1)
                nc.gpsimd.tensor_tensor(xs_lo[p][:], xs_in[p][:], xs_hi[p][:].bitcast(F32), ALU.subtract).then_inc(xs_lo_done, 1)

            def step(t, p, s, a, b, c, f, d):
                q = 1 - p
                if a:
                    pool.wait_ge(ln_done[0], t + 2)
                    wait(pool, g_done, t)
                    norm(0, xnT[q], xT, range(norm1_split(t + 1), CHUNKS), norm1_done)
                if d and (not isinstance(t, int) or t < IMAGES + 2):
                    pool.wait_ge(norm2_first, t - 2)
                    pool.wait_ge(norm2_last, t - 2)
                    wait(pool, feat_done, t - 3)
                    nc.gpsimd.tensor_tensor(feat[:], feat[:], xn2T[:], ALU.add).then_inc(feat_done, 1)
                if at(t, IMAGES - 1):
                    split_low(0, 0)
                if f:
                    statistics(1, t - 2)
                    pool.wait_ge(ln_done[1], t - 1)
                    wait(pool, xn2t_done, t - 2)
                    wait(pool, feat_done, t - 2)
                    norm(1, xn2T, x1_tokens(t - 2), range(norm2_split(t - 2), CHUNKS), norm2_last)
                if s:
                    wait(pool, norm1_done, t + 2)
                    statistics(0, t + 2)

            rounds(pool, step)
            def bias_x1(b, p):
                pool.wait_ge(x1_loaded[p], 8 * b + (8 if p else 16))
                nc.gpsimd.tensor_tensor(x_res[p][:], x_res[p][:], bias_out, ALU.add).then_inc(x1_biased, 1)

            def finish(b, p):
                pool.wait_ge(y_out_moved, b + 1)
                pool.wait_ge(x1_biased, b + 1)
                nc.gpsimd.tensor_tensor(x_res[p][:], y_out[:], x_res[p][:], ALU.add).then_inc(out_done, 1)

            for t in range(IMAGES, IMAGES + 3):
                last_round(step, t)
            pool.wait_ge(bias_moved, 1)
            bias_x1(0, 0)
            with pool.Fori(0, IMAGES // 2 - 1) as i:
                for p in (1, 0):
                    split_low(2 * i + (1 if p else 2), p)
                    finish(2 * i + (0 if p else 1), 1 - p)
                    bias_x1(2 * i + (1 if p else 2), p)
            split_low(IMAGES - 1, 1)
            finish(IMAGES - 2, 0)
            bias_x1(IMAGES - 1, 1)




def kernel(x, L0_conv_w_qkv, L0_conv_w_out, L0_conv_b_out, L0_ffn_Wr, L0_ffn_br, L0_ffn_W1, L0_ffn_b1, L0_ffn_g1,
           L0_ffn_be1, L0_ffn_m1, L0_ffn_v1, L0_ffn_W2, L0_ffn_b2, L0_ffn_g2, L0_ffn_be2, L0_ffn_m2, L0_ffn_v2,
           L0_ffn_Wo, L0_ffn_bo):
    import concourse.bacc as bacc
    from concourse.bass_utils import run_bass_kernel_spmd as run

    small = np.stack([np.asarray(a) for a in (
        L0_ffn_g1, L0_ffn_v1, L0_ffn_b1, L0_ffn_m1, L0_ffn_be1,
        L0_ffn_g2, L0_ffn_v2, L0_ffn_b2, L0_ffn_m2, L0_ffn_be2)]).transpose(2, 0, 1)
    arrays = {
        "x": np.asarray(x).reshape(IMAGES, C, PIXELS),
        "w_qkv": np.asarray(L0_conv_w_qkv),
        "w_out": np.asarray(L0_conv_w_out),
        "b_out": np.asarray(L0_conv_b_out).reshape(C, 1),
        "Wr": np.asarray(L0_ffn_Wr),
        "br": np.ascontiguousarray(np.broadcast_to(np.asarray(L0_ffn_br)[None, :], (128, EXPERTS))),
        "W1": np.asarray(L0_ffn_W1),
        "W2": np.asarray(L0_ffn_W2),
        "Wo": np.asarray(L0_ffn_Wo),
        "small": np.ascontiguousarray(small),
        "bo": np.asarray(L0_ffn_bo),
        "ident": np.eye(128, dtype=np.float32),
        "heads": np.kron(np.eye(128 // HEAD_DIM), np.ones((HEAD_DIM, HEAD_DIM))).astype(np.float32),
    }
    nc = bacc.Bacc("TRN2", target_bir_lowering=False, num_devices=1)
    arrays = {f"in_{name}": np.ascontiguousarray(a) for name, a in arrays.items()}
    args = [nc.dram_tensor(name, a.shape, F32, kind="ExternalInput").ap() for name, a in arrays.items()]
    out = nc.dram_tensor("out_0", [IMAGES, C, PIXELS], F32, kind="ExternalOutput").ap()
    metaformer_kernel(nc, *args, out)
    result = run(nc, [arrays], core_ids=[0]).results[0]["out_0"]
    return result.reshape(IMAGES, C, SIDE, SIDE)
```
